# Optimizing a Trainium2 kernel written in Bass

```python
import numpy as np
import jax
import jax.numpy as jnp

def _softmax(x, axis=-1):
    return jax.nn.softmax(x, axis=axis)

def _gelu(x):
    return jax.nn.gelu(x, approximate=True)

def _silu(x):
    return jax.nn.silu(x)

def _sigmoid(x):
    return jax.nn.sigmoid(x)

def _layernorm(x, axis=-1, eps=1e-05):
    m = jnp.mean(x, axis=axis, keepdims=True)
    v = jnp.var(x, axis=axis, keepdims=True)
    return (x - m) / jnp.sqrt(v + eps)

def _scatter_add(tgt, idx, src, axis=0):
    return tgt.at[idx].add(src)

def _segment_sum(src, seg, n):
    return jax.ops.segment_sum(src, seg, n)
kernel_name = 'mk_decoder_preln_d1_seqx_r4_ad7e61'

def setup_inputs(seed: int=0):
    np.random.seed(seed)
    _w = jnp.asarray

    def _rec_inputs():
        import jax
        import jax.numpy as jnp
        _rk = jax.random.key(seed)
        x = 0.0003765 + 1 * jax.random.normal(jax.random.fold_in(_rk, 1), (8, 256, 512), jnp.float32)
        _lenS = 256 - jax.random.randint(jax.random.fold_in(_rk, 7), (8,), 0, max(1, 256 // 4) + 1, jnp.int32)
        _lenS2 = 256 - jax.random.randint(jax.random.fold_in(_rk, 8), (8,), 0, max(1, 256 // 4) + 1, jnp.int32)
        _ctx_2048P = jax.random.normal(jax.random.fold_in(_rk, 11), (8, 16, 512), jnp.float32)
        _ctx_2048c = jax.random.dirichlet(jax.random.fold_in(_rk, 511), 0.3 * jnp.ones((16,), jnp.float32), (8, 256))
        _ctx_2048t = jnp.einsum('bsk,bkd->bsd', _ctx_2048c, _ctx_2048P)
        _ctx_2048t = _ctx_2048t * jax.lax.rsqrt(jnp.mean(jnp.square(_ctx_2048t)) + 1e-12) * 0.953939
        ctx_2048 = -0.000292821 + 1.00034 * (_ctx_2048t + 0.3 * jax.random.normal(jax.random.fold_in(_rk, 611), (8, 256, 512), jnp.float32))
        return (x, ctx_2048)
    x, ctx_2048 = _rec_inputs()

    def _L0_attn_setup():
        import jax, jax.numpy as jnp
        import numpy as np
        import math
        HID = 512
        HEADS = 16
        HEAD_DIM = HID // HEADS
        SEQ = 1024
        BATCH = 1
        ROPE_THETA = 10000.0
        START_RATIO = 0.1
        RECENT_RATIO = 0.25

        def _rope_sin_cos(seq_len, dtype):
            theta = 1.0 / ROPE_THETA ** (jnp.arange(0, HEAD_DIM, 2, dtype=jnp.float32) / HEAD_DIM)
            sinusoid = jnp.arange(seq_len, dtype=jnp.float32)[:, None] * theta[None, :]
            return (jnp.sin(sinusoid).astype(dtype), jnp.cos(sinusoid).astype(dtype))

        def _apply_rope(x, sin, cos):
            x1, x2 = (x[..., 0::2], x[..., 1::2])
            return jnp.concatenate([x1 * cos - x2 * sin, x1 * sin + x2 * cos], axis=-1)
        key = jax.random.key(seed)
        ks = jax.random.split(key, 9)
        s = 0.02
        return {'hidden_states': jax.random.normal(ks[0], (BATCH, SEQ, HID), jnp.float32), 'Wq': jax.random.normal(ks[1], (HID, HID), jnp.float32) * s, 'bq': jnp.zeros((HID,), jnp.float32), 'Wk': jax.random.normal(ks[2], (HID, HID), jnp.float32) * s, 'bk': jnp.zeros((HID,), jnp.float32), 'Wv': jax.random.normal(ks[3], (HID, HID), jnp.float32) * s, 'bv': jnp.zeros((HID,), jnp.float32), 'Wo': jax.random.normal(ks[4], (HID, HID), jnp.float32) * s, 'bo': jnp.zeros((HID,), jnp.float32)}
    _L0_attn_all = _L0_attn_setup()
    _L0_attn_in = {k: v for k, v in _L0_attn_all.items() if k in ('Wq', 'bq', 'Wk', 'bk', 'Wv', 'bv', 'Wo', 'bo')}
    del _L0_attn_all

    def _L0_xattn_setup():
        import jax, jax.numpy as jnp
        import numpy as np
        key = jax.random.key(seed)
        k1, k2, k3, k4, k5 = jax.random.split(key, 5)
        B, D_MODEL, L = (2, 256, 512)
        HEAD_DIM = 8
        H = D_MODEL // HEAD_DIM
        return {'k': jax.random.normal(k1, (B, D_MODEL, L), dtype=jnp.float32), 'v': jax.random.normal(k2, (B, D_MODEL, L), dtype=jnp.float32), 'q': jax.random.normal(k3, (B, D_MODEL, L), dtype=jnp.float32), 'ssm_kernel': jax.random.normal(k4, (H, L), dtype=jnp.float32), 'D': jax.random.normal(k5, (H,), dtype=jnp.float32), 'head_dim': HEAD_DIM}
    _L0_xattn_all = _L0_xattn_setup()
    _L0_xattn_in = {k: v for k, v in _L0_xattn_all.items() if k in ('ssm_kernel', 'D')}
    del _L0_xattn_all

    def _L0_ffn_setup():
        import jax, jax.numpy as jnp
        import numpy as np
        E, K = (12, 3)
        B, S, H, I = (2, 512, 512, 1280)

        def _forward(x, Wr, br, w1, b1, w2, b2, Wp1, bp1, Wp2, bp2):
            logits = jnp.einsum('bsh,he->bse', x, Wr) + br
            probs = jax.nn.softmax(logits, axis=-1)
            top_vals, top_idx = jax.lax.top_k(probs, K)
            ew = jax.nn.softmax(top_vals, axis=-1)
            out = jnp.zeros_like(x)
            for e in range(E):
                sel = top_idx == e
                mask = sel.any(axis=-1)
                cnt = sel.sum()
                w_e = jnp.sum(jnp.where(sel, ew, 0.0)) / jnp.maximum(cnt, 1).astype(ew.dtype)
                h = jax.nn.relu(jnp.einsum('bsh,hi->bsi', x, w1[e]) + b1[e])
                h = jnp.einsum('bsi,ih->bsh', h, w2[e]) + b2[e]
                out = out + mask[..., None].astype(x.dtype) * (w_e * h)
            pooled = out.mean(axis=1)
            phi = jax.nn.sigmoid(jax.nn.relu(pooled @ Wp1 + bp1) @ Wp2 + bp2)
            phi_mask = (phi > 0.7).astype(out.dtype)[:, :, None]
            return out * (1.0 - phi_mask * 0.8)
        key = jax.random.key(seed)
        ks = jax.random.split(key, 8)
        sH = np.float32(1.0 / np.sqrt(H))
        sI = np.float32(1.0 / np.sqrt(I))
        sH2 = np.float32(1.0 / np.sqrt(H // 2))
        return {'hidden_states': jax.random.normal(ks[0], (B, S, H), jnp.float32), 'Wr': jax.random.normal(ks[1], (H, E), jnp.float32) * sH, 'br': jnp.zeros((E,), jnp.float32), 'w1': jax.random.normal(ks[2], (E, H, I), jnp.float32) * sH, 'b1': jnp.zeros((E, I), jnp.float32), 'w2': jax.random.normal(ks[3], (E, I, H), jnp.float32) * sI, 'b2': jnp.zeros((E, H), jnp.float32), 'Wp1': jax.random.normal(ks[4], (H, H // 2), jnp.float32) * sH, 'bp1': jnp.zeros((H // 2,), jnp.float32), 'Wp2': jax.random.normal(ks[5], (H // 2, 1), jnp.float32) * sH2, 'bp2': jnp.zeros((1,), jnp.float32)}
    _L0_ffn_all = _L0_ffn_setup()
    _L0_ffn_in = {k: v for k, v in _L0_ffn_all.items() if k in ('Wr', 'br', 'w1', 'b1', 'w2', 'b2', 'Wp1', 'bp1', 'Wp2', 'bp2')}
    del _L0_ffn_all
    return {'x': x, 'ctx_2048': ctx_2048, 'L0_attn_Wq': _L0_attn_in['Wq'], 'L0_attn_bq': _L0_attn_in['bq'], 'L0_attn_Wk': _L0_attn_in['Wk'], 'L0_attn_bk': _L0_attn_in['bk'], 'L0_attn_Wv': _L0_attn_in['Wv'], 'L0_attn_bv': _L0_attn_in['bv'], 'L0_attn_Wo': _L0_attn_in['Wo'], 'L0_attn_bo': _L0_attn_in['bo'], 'L0_xattn_ssm_kernel': _L0_xattn_in['ssm_kernel'], 'L0_xattn_D': _L0_xattn_in['D'], 'L0_ffn_Wr': _L0_ffn_in['Wr'], 'L0_ffn_br': _L0_ffn_in['br'], 'L0_ffn_w1': _L0_ffn_in['w1'], 'L0_ffn_b1': _L0_ffn_in['b1'], 'L0_ffn_w2': _L0_ffn_in['w2'], 'L0_ffn_b2': _L0_ffn_in['b2'], 'L0_ffn_Wp1': _L0_ffn_in['Wp1'], 'L0_ffn_bp1': _L0_ffn_in['bp1'], 'L0_ffn_Wp2': _L0_ffn_in['Wp2'], 'L0_ffn_bp2': _L0_ffn_in['bp2']}

def reference(x, ctx_2048, L0_attn_Wq, L0_attn_bq, L0_attn_Wk, L0_attn_bk, L0_attn_Wv, L0_attn_bv, L0_attn_Wo, L0_attn_bo, L0_xattn_ssm_kernel, L0_xattn_D, L0_ffn_Wr, L0_ffn_br, L0_ffn_w1, L0_ffn_b1, L0_ffn_w2, L0_ffn_b2, L0_ffn_Wp1, L0_ffn_bp1, L0_ffn_Wp2, L0_ffn_bp2):
    import jax
    import jax.numpy as jnp

    def _L0_attn_ref(hidden_states, Wq, bq, Wk, bk, Wv, bv, Wo, bo):
        import jax, jax.numpy as jnp
        import numpy as np
        import math
        HID = 512
        HEADS = 16
        HEAD_DIM = HID // HEADS
        SEQ = 1024
        BATCH = 1
        ROPE_THETA = 10000.0
        START_RATIO = 0.1
        RECENT_RATIO = 0.25

        def _rope_sin_cos(seq_len, dtype):
            theta = 1.0 / ROPE_THETA ** (jnp.arange(0, HEAD_DIM, 2, dtype=jnp.float32) / HEAD_DIM)
            sinusoid = jnp.arange(seq_len, dtype=jnp.float32)[:, None] * theta[None, :]
            return (jnp.sin(sinusoid).astype(dtype), jnp.cos(sinusoid).astype(dtype))

        def _apply_rope(x, sin, cos):
            x1, x2 = (x[..., 0::2], x[..., 1::2])
            return jnp.concatenate([x1 * cos - x2 * sin, x1 * sin + x2 * cos], axis=-1)
        b, s, _ = hidden_states.shape

        def proj(W, bias):
            y = jnp.einsum('bsd,ed->bse', hidden_states, W) + bias
            return y.reshape(b, s, HEADS, HEAD_DIM).transpose(0, 2, 1, 3)
        q = proj(Wq, bq)
        k = proj(Wk, bk)
        v = proj(Wv, bv)
        sin, cos = _rope_sin_cos(s, hidden_states.dtype)
        q = _apply_rope(q, sin, cos)
        k = _apply_rope(k, sin, cos)
        scale = 1.0 / math.sqrt(HEAD_DIM)
        scores = jnp.einsum('bhqd,bhkd->bhqk', q, k) * scale
        start_budget = math.ceil(START_RATIO * s)
        recent_budget = math.ceil(RECENT_RATIO * s)
        pos = np.arange(s)
        cam = jnp.asarray((pos < start_budget) | (pos >= s - recent_budget))
        neg = jnp.finfo(scores.dtype).min
        scores = jnp.where(cam[None, None, None, :], scores, neg)
        attn = jax.nn.softmax(scores, axis=-1)
        out = jnp.einsum('bhqk,bhkd->bhqd', attn, v)
        out = out.transpose(0, 2, 1, 3).reshape(b, s, HID)
        return jnp.einsum('bsd,ed->bse', out, Wo) + bo

    def _L0_xattn_ref(k, v, q, ssm_kernel, D, head_dim):
        import jax, jax.numpy as jnp
        import numpy as np
        B, HD, L = k.shape
        H = HD // head_dim
        fft_size = 2 * L
        k_ = k.reshape(B, H, head_dim, L)
        v_ = v.reshape(B, H, head_dim, L)
        q_ = q.reshape(B, H, head_dim, L)
        kv = jnp.einsum('bhil,bhjl->bijhl', k_, v_)
        kv_f = jnp.fft.rfft(kv, n=fft_size)
        kernel_f = jnp.fft.rfft(ssm_kernel, n=fft_size)
        y = jnp.fft.irfft(kv_f * kernel_f, n=fft_size)[..., :L]
        out = y + kv * D[None, None, None, :, None]
        out = jnp.einsum('bijhl,bhil->bjhl', out, q_)
        out = jnp.transpose(out, (0, 2, 1, 3)).reshape(B, H * head_dim, L)
        return out.astype(k.dtype)

    def _L0_ffn_ref(hidden_states, Wr, br, w1, b1, w2, b2, Wp1, bp1, Wp2, bp2):
        import jax, jax.numpy as jnp
        import numpy as np
        E, K = (12, 3)
        B, S, H, I = (2, 512, 512, 1280)

        def _forward(x, Wr, br, w1, b1, w2, b2, Wp1, bp1, Wp2, bp2):
            logits = jnp.einsum('bsh,he->bse', x, Wr) + br
            probs = jax.nn.softmax(logits, axis=-1)
            top_vals, top_idx = jax.lax.top_k(probs, K)
            ew = jax.nn.softmax(top_vals, axis=-1)
            out = jnp.zeros_like(x)
            for e in range(E):
                sel = top_idx == e
                mask = sel.any(axis=-1)
                cnt = sel.sum()
                w_e = jnp.sum(jnp.where(sel, ew, 0.0)) / jnp.maximum(cnt, 1).astype(ew.dtype)
                h = jax.nn.relu(jnp.einsum('bsh,hi->bsi', x, w1[e]) + b1[e])
                h = jnp.einsum('bsi,ih->bsh', h, w2[e]) + b2[e]
                out = out + mask[..., None].astype(x.dtype) * (w_e * h)
            pooled = out.mean(axis=1)
            phi = jax.nn.sigmoid(jax.nn.relu(pooled @ Wp1 + bp1) @ Wp2 + bp2)
            phi_mask = (phi > 0.7).astype(out.dtype)[:, :, None]
            return out * (1.0 - phi_mask * 0.8)
        return _forward(hidden_states, Wr, br, w1, b1, w2, b2, Wp1, bp1, Wp2, bp2)
    x = x + _L0_attn_ref(_layernorm(x, axis=-1), L0_attn_Wq, L0_attn_bq, L0_attn_Wk, L0_attn_bk, L0_attn_Wv, L0_attn_bv, L0_attn_Wo, L0_attn_bo)
    x = x + _L0_xattn_ref(ctx_2048, ctx_2048, _layernorm(x, axis=-1), L0_xattn_ssm_kernel, L0_xattn_D, 8)
    x = x + _L0_ffn_ref(_layernorm(x, axis=-1), L0_ffn_Wr, L0_ffn_br, L0_ffn_w1, L0_ffn_b1, L0_ffn_w2, L0_ffn_b2, L0_ffn_Wp1, L0_ffn_bp1, L0_ffn_Wp2, L0_ffn_bp2)
    return x

_drawn_inputs = setup_inputs


def setup_inputs(seed=0):
    import zlib

    import numpy as np

    out = dict(_drawn_inputs(seed))
    spreads = {'L0_attn_bq': (0.0, 0.8),
     'L0_attn_bk': (0.0, 0.8),
     'L0_attn_bv': (0.0, 0.1),
     'L0_attn_bo': (0.0, 0.1),
     'L0_ffn_br': (0.0, 0.8),
     'L0_ffn_b1': (0.0, 0.8),
     'L0_ffn_b2': (0.0, 0.8),
     'L0_ffn_bp1': (0.0, 0.1)}
    factors = {'L0_attn_Wq': 8.0,
     'L0_attn_Wk': 8.0,
     'L0_ffn_Wr': 8.0,
     'L0_ffn_w1': 8.0,
     'L0_ffn_w2': 7.665}
    for name, (base, spread) in spreads.items():
        noise = np.random.default_rng([zlib.crc32(name.encode()), seed]).standard_normal(out[name].shape)
        drawn = base * np.exp(spread * noise) if base else spread * noise
        out[name] = jnp.asarray(drawn.astype(out[name].dtype))
    for name, factor in factors.items():
        out[name] = (out[name] * factor).astype(out[name].dtype)
    return out
```

```python
from contextlib import ExitStack

import concourse.bass as bass
from concourse import mybir

F32 = mybir.dt.float32
F32R = mybir.dt.float32r
I32 = mybir.dt.int32
U32 = mybir.dt.uint32
ACT = mybir.ActivationFunctionType
ALU = mybir.AluOpType
AX_X = mybir.AxisListType.X

P = 128
B, S, D = 8, 256, 512
KD = D // P
TPB = S // P
NT = B * TPB
HEADS = 16
HD = D // HEADS
START, RECENT = 26, 64
NK = START + RECENT
SCALE = float(HD) ** -0.5
EPS = 1e-5

SH = 32
CH = 8
LB = D // P
ND = 5
CE = CH + ND - 1
QE = 2 * CH
KPAD = 640

E, TOPK = 12, 3
FF = 1280
KF = FF // P
NTILE = NT * TOPK + E
TRASH = NT * P

C_ID = 0
C_UP = C_ID + P
C_ONE = C_UP + P
C_IOTA = C_ONE + P
C_ROPE = C_IOTA + P
C_LOW = C_ROPE + 3 * HD
C_TOK = C_LOW + E * E
C_TRASH = C_TOK + NT
NCONST = C_TRASH + 1


def view(ap, off, dims):
    return bass.AP(tensor=ap.tensor, offset=ap.offset + off, ap=[ap.ap[0]] + [list(d) for d in dims])


def bc(ap, n):
    return bass.AP(tensor=ap.tensor, offset=ap.offset, ap=[list(d) for d in ap.ap] + [[0, n]])


class Steps:

    def __init__(self, eng, sem, base=0):
        self.eng, self.sem, self.base, self.n = eng, sem, base, 0

    def do(self, ins):
        self.n += 1
        ins.then_inc(self.sem, 1)
        self.eng.wait_ge(self.sem, self.base + self.n)


def attention(nc, xs, cst, x, wqT, wkT, wvT, woT, bq, bk, bv, bo, consts, stats1):
    with ExitStack() as ctx:
        def sb(name, shape, dt=F32):
            return ctx.enter_context(nc.sbuf_tensor(name, shape, dt))

        def psum(name, shape):
            return ctx.enter_context(nc.psum_tensor(name, shape, F32))

        def sem(name):
            return ctx.enter_context(nc.semaphore(name))

        wq, wk, wv, wo = (sb(n, [P, KD * D]) for n in ("wq", "wk", "wv", "wo"))
        bias_q, bias_k, bias_v, bias_o = (sb(n, [P, D]) for n in ("bias_q", "bias_k", "bias_v", "bias_o"))
        stats = sb("stats", [P, NT, 6])
        mv = sb("mv", [P, NT, 2])
        rstd = sb("rstd", [P, NT])
        xn = sb("xn", [P, TPB, D])
        xT = sb("xT", [P, TPB, KD, P])
        xkT = sb("xkT", [P, KD, NK])
        qkb = sb("qkb", [P, 3, D])
        rc = sb("rc", [P, D])
        rs = sb("rs", [P, D])
        qkr = sb("qkr", [P, 3, D])
        qT = sb("qT", [P, TPB, KD, P])
        kT = sb("kT", [P, KD, NK])
        vv = sb("vv", [NK, D])
        mx = sb("mx", [P, HEADS])
        sx = sb("sx", [P, TPB, HEADS * NK])
        pm = sb("pm", [P, TPB, HEADS * NK])
        den = sb("den", [P, TPB, HEADS])
        rden = sb("rden", [P, TPB, HEADS])
        pT = sb("pT", [NK, HEADS * P])
        oo = sb("oo", [P, D])
        oT = sb("oT", [P, KD, P])
        yo = sb("yo", [P, D])

        ps_t = psum("ps_t", [P, 512])
        ps_p = psum("ps_p", [P, 2, 512])
        ps_s = psum("ps_s", [P, 4, 512])
        ps_o = psum("ps_o", [P, 512])

        x_in = [sem(f"x_in{i}") for i in range(4)]
        c_in, wq_in, wk_in, wv_in, wo_in, b_in = (sem(n) for n in ("c_in", "wq_in", "wk_in", "wv_in", "wo_in", "b_in"))
        var_ready = sem("var_ready")
        std_ready = sem("std_ready")
        xn_ready = sem("xn_ready")
        xt_done = sem("xt_done")
        qkt_done = sem("qkt_done")
        ot_done = sem("ot_done")
        t_evac = sem("t_evac")
        qkv_done = sem("qkv_done")
        wo_done = sem("wo_done")
        p_evac = sem("p_evac")
        roped = sem("roped")
        s_done = sem("s_done")
        sx_ready = sem("sx_ready")
        exp_done = sem("exp_done")
        pt_done = sem("pt_done")
        pt_evac = sem("pt_evac")
        pv_done = sem("pv_done")
        o_ready = sem("o_ready")
        dve_step = sem("dve_step")
        pool_step = sem("pool_step")
        stats_done = sem("stats_done")
        aggr_done = sem("aggr_done")

        def t_xt(b, t):
            return 5 + 7 * (b - 1) + t if not isinstance(b, int) or b else t

        def t_qk(b, j):
            return 5 + 7 * (b - 1) + 3 + j if not isinstance(b, int) or b else 2 + j

        def t_ot(b, t, last):
            return 5 + 7 * b + (t if last else (2, 6)[t])

        def p_qkv(b, j):
            return 4 + 6 * (b - 1) + (0, 1, 2, 4)[j] if not isinstance(b, int) or b else j

        def p_wo(b, t, last):
            return 4 + 6 * b + (t if last else (3, 5)[t])

        bank_qkv0, bank_qkv, bank_wo, bank_wo_last = (0, 1, 0, 1), (0, 1, 0, 0), (1, 1), (0, 1)

        block = ctx.enter_context(nc.Block())

        @block.sync
        def _(sp):
            xt = x.rearrange("b (t p) d -> p (b t) d", p=P)
            for i in range(4):
                sp.dma_start(xs[:, 4 * i:4 * i + 4, :], xt[:, 4 * i:4 * i + 4, :]).then_inc(x_in[i], 16)
            sp.dma_start(wo[:].rearrange("p (k n) -> p k n", k=KD),
                         woT.rearrange("(k p) n -> p k n", p=P)).then_inc(wo_in, 16)

        @block.scalar
        def _(act):
            act.dma_start(cst[:], consts).then_inc(c_in, 16)
            for w, src, s in ((wq, wqT, wq_in), (wk, wkT, wk_in), (wv, wvT, wv_in)):
                act.dma_start(w[:].rearrange("p (k n) -> p k n", k=KD),
                              src.rearrange("(k p) n -> p k n", p=P)).then_inc(s, 16)
            for t, src in ((bias_q, bq), (bias_k, bk), (bias_v, bv), (bias_o, bo)):
                act.dma_start(t[:], src.partition_broadcast(P)).then_inc(b_in, 16)
            act.wait_ge(var_ready, 1)
            nc.scalar.activation(rstd[:], rstd[:], ACT.Sqrt).then_inc(std_ready, 1)

            act.sem_inc(pt_evac, 1)

            def evac(done, n, dst, src):
                act.wait_ge(done, n)
                nc.scalar.activation(dst, src, ACT.Copy).then_inc(t_evac, 1)

            def evac_x(b, t):
                lo, hi, at = ((0, START, 0), (P - RECENT, P, START))[t]
                act.wait_ge(xt_done, 2 * b + t + 1)
                ps = ps_t[:].rearrange("p (k n) -> p k n", k=KD)
                nc.scalar.activation(xkT[:, :, at:at + hi - lo], ps[:, :, lo:hi], ACT.Copy)
                nc.scalar.activation(xT[:, t], ps, ACT.Copy).then_inc(t_evac, 1)

            def evac_qk(b):
                for t in range(TPB):
                    evac(qkt_done, 3 * b + t + 1, qT[:, t].rearrange("p k n -> p (k n)"), ps_t[:])
                evac(qkt_done, 3 * b + 3, kT[:], ps_t[:].rearrange("p (k n) -> p k n", k=KD)[:, :, 0:NK])

            def exps(b, t):
                act.wait_ge(sx_ready, 2 * b + t + 1)
                nc.scalar.activation(pm[:, t], sx[:, t], ACT.Exp, scale=SCALE).then_inc(exp_done, 1)

            def evac_pt(b, t):
                act.wait_ge(pt_done, 2 * b + t + 1)
                act.wait_ge(pv_done, 2 * b + t + 1)
                nc.scalar.activation(pT[:].rearrange("p (g n) -> p g n", g=4), ps_s[0:NK], ACT.Copy)\
                    .then_inc(pt_evac, 1)

            def batch(b, last):
                if not last:
                    evac_x(b + 1, 0)
                    evac_x(b + 1, 1)
                exps(b, 0)
                evac_pt(b, 0)
                evac(ot_done, 2 * b + 2, oT[:].rearrange("p k n -> p (k n)"), ps_t[:])
                exps(b, 1)
                if not last:
                    evac_qk(b + 1)
                evac_pt(b, 1)
                evac(ot_done, 2 * b + 3, oT[:].rearrange("p k n -> p (k n)"), ps_t[:])

            evac_x(0, 0)
            evac_x(0, 1)
            evac_qk(0)
            with act.Fori(0, B - 1) as b:
                batch(b, False)
            batch(B - 1, True)

        @block.gpsimd
        def _(pool):
            def rope(b, j, steps):
                idx = p_qkv(b, j)
                pool.wait_ge(p_evac, idx + 1)
                if not isinstance(b, int) or b:
                    pool.wait_ge(qkt_done, 3 * b + j - 2)
                n = P if j < 2 else NK
                src = qkb[0:n, j]
                out = qkr[0:n, j]
                cos = view(cst[0:n], C_ROPE + j * HD, [[0, HEADS], [1, HD // 2], [0, 2]])
                sin = view(cst[0:n], C_ROPE + j * HD + HD // 2, [[0, HEADS], [1, HD // 2]])

                def pair(a, k):
                    return view(a, k, [[HD, HEADS], [2, HD // 2]])

                def full(a):
                    return view(a, 0, [[HD, HEADS], [2, HD // 2], [1, 2]])

                nc.gpsimd.tensor_tensor(pair(rs[0:n], 0), pair(src, 1), sin, ALU.mult)
                nc.gpsimd.tensor_tensor(pair(rs[0:n], 1), pair(src, 0), sin, ALU.mult)
                steps.do(nc.gpsimd.tensor_tensor(full(rc[0:n]), full(src), cos, ALU.mult))
                nc.gpsimd.tensor_tensor(pair(out, 0), pair(rc[0:n], 0), pair(rs[0:n], 0), ALU.subtract)
                nc.gpsimd.tensor_tensor(pair(out, 1), pair(rc[0:n], 1), pair(rs[0:n], 1), ALU.add)\
                    .then_inc(roped, 1)
                pool.wait_ge(roped, roped_index(b, j) + 1)

            def roped_index(b, j):
                return 3 * b + j

            pool.wait_ge(c_in, 16)
            first = Steps(pool, pool_step)
            for j in range(3):
                rope(0, j, first)
            with pool.Fori(0, B - 1) as b:
                loop = Steps(pool, pool_step, base=first.n + 3 * b)
                for j in range(3):
                    rope(b + 1, j, loop)

        @block.vector
        def _(dve):
            dve.sem_inc(o_ready, 1)
            for i in range(4):
                dve.wait_ge(x_in[i], 16)
                with dve.Fori(4 * i, 4 * i + 4) as t:
                    nc.vector.bn_stats(stats[:, t], xs[:, t]).then_inc(stats_done, 1)
            dve.wait_ge(stats_done, NT)
            for t in range(NT):
                nc.vector.bn_aggr(mv[:, t], stats[:, t]).then_inc(aggr_done, 1)
            dve.wait_ge(aggr_done, NT)
            steps = Steps(dve, dve_step)
            nc.vector.tensor_scalar(rstd[:], mv[:, :, 1], EPS, None, ALU.add).then_inc(var_ready, 1)
            dve.wait_ge(std_ready, 1)
            steps.do(nc.vector.reciprocal(rstd[:], rstd[:]))
            dve.wait_ge(b_in, 64)

            def normalise(b, t):
                if not isinstance(b, int) or b:
                    dve.wait_ge(xt_done, 2 * b + t - 1)
                i = 2 * b + t
                nc.vector.tensor_scalar(xn[:, t], xs[:, i], mv[:, i, 0:1], rstd[:, bass.ds(i, 1)],
                                        ALU.subtract, ALU.mult).then_inc(xn_ready, 1)

            def add_bias(b, j, bank):
                dve.wait_ge(qkv_done, 4 * b + j + 1)
                n = P if j < 2 else NK
                if j < 3 and (not isinstance(b, int) or b):
                    dve.wait_ge(roped, 3 * b + j - 2)
                dst = vv[:] if j == 3 else qkb[0:n, j]
                bias = (bias_q, bias_q, bias_k, bias_v)[j]
                nc.vector.tensor_tensor(dst, ps_p[0:n, bank], bias[0:n], ALU.add).then_inc(p_evac, 1)

            def softmax_top(b, t, steps):
                dve.wait_ge(s_done, 2 * b + t + 1)
                sc = view(ps_s[:], 0, [[512, 4], [NK, 4], [1, NK]])
                steps.do(nc.vector.tensor_reduce(mx[:].rearrange("p (g h) -> p g h", g=4), sc, AX_X, ALU.max))
                mxb = view(mx[:], 0, [[4, 4], [1, 4], [0, NK]])
                nc.vector.tensor_tensor(view(sx[:, t], 0, [[4 * NK, 4], [NK, 4], [1, NK]]), sc, mxb,
                                        ALU.subtract).then_inc(sx_ready, 1)
                dve.wait_ge(sx_ready, 2 * b + t + 1)

            def softmax_sum(b, t, steps):
                dve.wait_ge(exp_done, 2 * b + t + 1)
                steps.do(nc.vector.tensor_reduce(den[:, t], view(pm[:, t], 0, [[NK, HEADS], [1, NK]]),
                                                 AX_X, ALU.add))
                steps.do(nc.vector.reciprocal(rden[:, t], den[:, t]))

            def divide(b, t):
                dve.wait_ge(pv_done, 2 * b + t + 2)
                dve.wait_ge(ot_done, 2 * b + t + 1)
                heads = [[4 * HD, 4], [HD, 4], [1, HD]]
                nc.vector.tensor_tensor(view(oo[:], 0, heads), view(ps_o[:], 0, heads),
                                        view(rden[:, t], 0, [[1, 4], [4, 4], [0, HD]]), ALU.mult)\
                    .then_inc(o_ready, 1)

            def residual(b, t, last, steps):
                dve.wait_ge(wo_done, 2 * b + t + 1)
                i = 2 * b + t
                bank = (bank_wo_last if last else bank_wo)[t]
                ins = nc.vector.tensor_tensor(yo[:], ps_p[:, bank], bias_o[:], ALU.add)
                ins.then_inc(p_evac, 1)
                dve.wait_ge(p_evac, p_wo(b, t, last) + 1)
                steps.do(nc.vector.tensor_tensor(xs[:, i], xs[:, i], yo[:], ALU.add))
                nc.vector.bn_stats(stats1[:, i], xs[:, i])

            def batch(b, last, steps):
                if not last:
                    normalise(b + 1, 0)
                    normalise(b + 1, 1)
                softmax_top(b, 0, steps)
                if not last:
                    add_bias(b + 1, 0, bank_qkv[0])
                softmax_sum(b, 0, steps)
                divide(b, 0)
                if not last:
                    add_bias(b + 1, 1, bank_qkv[1])
                    add_bias(b + 1, 2, bank_qkv[2])
                softmax_top(b, 1, steps)
                residual(b, 0, last, steps)
                softmax_sum(b, 1, steps)
                if not last:
                    add_bias(b + 1, 3, bank_qkv[3])
                divide(b, 1)
                residual(b, 1, last, steps)

            normalise(0, 0)
            normalise(0, 1)
            for j in range(4):
                add_bias(0, j, bank_qkv0[j])
            per_batch = 8
            with dve.Fori(0, B - 1) as b:
                loop = Steps(dve, dve_step, base=steps.n + per_batch * b)
                batch(b, False, loop)
            assert loop.n == per_batch, loop.n
            tail = Steps(dve, dve_step, base=steps.n + per_batch * (B - 1))
            batch(B - 1, True, tail)

        @block.tensor
        def _(pe):
            pe.wait_ge(c_in, 16)
            ident = cst[:, C_ID:C_ID + P]
            pe.sem_inc(pv_done, 1)
            pe.sem_inc(ot_done, 1)

            def free_t(idx):
                if not isinstance(idx, int) or idx:
                    pe.wait_ge(t_evac, idx)

            def free_p(idx):
                if not isinstance(idx, int) or idx > 1:
                    pe.wait_ge(p_evac, idx - 1)

            def transposes(idx, done, src, rows):
                free_t(idx)
                for k in range(KD):
                    last = nc.tensor.transpose(ps_t[:, k * P:k * P + rows], src[0:rows, k * P:(k + 1) * P],
                                               ident[0:rows, 0:rows])
                last.then_inc(done, 1)

            def x_t(b, t):
                pe.wait_ge(xn_ready, 2 * b + t + 1)
                transposes(t_xt(b, t), xt_done, xn[:, t], P)

            def qk_t(b):
                for j in range(3):
                    pe.wait_ge(roped, 3 * b + j + 1)
                    transposes(t_qk(b, j), qkt_done, qkr[:, j], P if j < 2 else NK)

            def o_t(b, t, last):
                pe.wait_ge(o_ready, 2 * b + t + 2)
                transposes(t_ot(b, t, last), ot_done, oo[:], P)

            def project(b, j, bank):
                free_p(p_qkv(b, j))
                pe.wait_ge(t_evac, t_xt(b, 1 if j else 0) + 1)
                w = (wq, wq, wk, wv)[j]
                n = P if j < 2 else NK
                for k in range(KD):
                    lhs = xT[:, j, k] if j < 2 else xkT[:, k]
                    last = nc.tensor.matmul(ps_p[0:n, bank], lhs, w[:, k * D:(k + 1) * D],
                                            start=(k == 0), stop=(k == KD - 1))
                last.then_inc(qkv_done, 1)

            def w_o(b, t, last):
                idx = p_wo(b, t, last)
                free_p(idx)
                pe.wait_ge(t_evac, t_ot(b, t, last) + 1)
                for k in range(KD):
                    mm = nc.tensor.matmul(ps_p[:, (bank_wo_last if last else bank_wo)[t]], oT[:, k],
                                          wo[:, k * D:(k + 1) * D], start=(k == 0), stop=(k == KD - 1))
                mm.then_inc(wo_done, 1)

            def scores(b, t):
                if t == 0:
                    pe.wait_ge(t_evac, 5 + 7 * b)
                pe.wait_ge(pt_evac, 2 * b + t + 1)
                for k in range(KD):
                    for g in range(4):
                        last = nc.tensor.matmul(ps_s[:, g, k * NK:(k + 1) * NK],
                                                qT[g * HD:(g + 1) * HD, t, k], kT[g * HD:(g + 1) * HD, k],
                                                start=True, stop=True)
                last.then_inc(s_done, 1)

            def p_t(b, t):
                pe.wait_ge(exp_done, 2 * b + t + 1)
                for h in range(HEADS):
                    last = nc.tensor.transpose(ps_s[0:NK, h // 4, (h % 4) * P:(h % 4 + 1) * P],
                                               pm[:, t, h * NK:(h + 1) * NK], ident)
                last.then_inc(pt_done, 1)

            def p_v(b, t):
                pe.wait_ge(pt_evac, 2 * b + t + 2)
                if t == 0:
                    pe.wait_ge(p_evac, 4 + 6 * b)
                pe.wait_ge(o_ready, 2 * b + t + 1)
                for h in range(HEADS):
                    head = 4 * (h % 4) + h // 4
                    last = nc.tensor.matmul(ps_o[:, head * HD:(head + 1) * HD], pT[:, h * P:(h + 1) * P],
                                            vv[:, head * HD:(head + 1) * HD], start=True, stop=True)
                last.then_inc(pv_done, 1)

            def batch(b, last):
                scores(b, 0)
                if not last:
                    x_t(b + 1, 0)
                    x_t(b + 1, 1)
                    project(b + 1, 0, bank_qkv[0])
                p_t(b, 0)
                p_v(b, 0)
                if not last:
                    project(b + 1, 1, bank_qkv[1])
                    project(b + 1, 2, bank_qkv[2])
                o_t(b, 0, last)
                scores(b, 1)
                w_o(b, 0, last)
                if not last:
                    qk_t(b + 1)
                p_t(b, 1)
                p_v(b, 1)
                if not last:
                    project(b + 1, 3, bank_qkv[3])
                o_t(b, 1, last)
                w_o(b, 1, last)

            x_t(0, 0)
            x_t(0, 1)
            pe.wait_ge(wq_in, 16)
            project(0, 0, bank_qkv0[0])
            project(0, 1, bank_qkv0[1])
            pe.wait_ge(wk_in, 16)
            project(0, 2, bank_qkv0[2])
            pe.wait_ge(wv_in, 16)
            project(0, 3, bank_qkv0[3])
            qk_t(0)
            pe.wait_ge(wo_in, 16)
            with pe.Fori(0, B - 1) as b:
                batch(b, False)
            batch(B - 1, True)


def convolution(nc, xs, cst, stats1, res, ctx_rev, taps, diag, kpad):
    with ExitStack() as ctx:
        def sb(name, shape, dt=F32):
            return ctx.enter_context(nc.sbuf_tensor(name, shape, dt))

        def psum(name, shape):
            return ctx.enter_context(nc.psum_tensor(name, shape, F32))

        def sem(name):
            return ctx.enter_context(nc.semaphore(name))

        NCOL = B * ND * CH
        mv = sb("mv_b", [P, NT, 2])
        rstd = sb("rstd_b", [P, NT])
        xn = sb("xn_b", [P, 2, D])
        qe = sb("qe", [P, LB * B * SH * QE])
        kp = sb("kp", [SH, KPAD])
        dd = sb("dd", [SH, 1])
        toe = sb("toe", [P, 2, D])
        cc = sb("cc", [P, 2, LB * B * CE])
        kv = sb("kv", [P, 2, LB * NCOL])
        ye = sb("ye", [P, 2, LB * B * ND * QE])
        prod = sb("prod", [P, LB * B * CH * CH])
        ps = psum("ps_b", [P, 8, 512])

        taps_in, pad_zero, pad_ready, pad_out = (sem(n) for n in ("taps_in", "pad_zero", "pad_ready", "pad_out"))
        aggr = sem("aggr_b")
        var_ready, std_ready = sem("var_ready_b"), sem("std_ready_b")
        dve_step = sem("dve_step_b")
        xn_ready = sem("xn_ready_b")
        xt_done = sem("xt_done_b")
        even_copied = sem("even_copied")
        odd_copied = sem("odd_copied")
        head_in = [sem("head_in0"), sem("head_in1")]
        kv_ready = sem("kv_ready")
        conv_done = sem("conv_done")
        ye_ready = sem("ye_ready")
        prod_ready = sem("prod_ready")
        res_ready = sem("res_ready")

        block = ctx.enter_context(nc.Block())

        @block.sync
        def _(sp):
            sp.dma_start(dd[:], diag.rearrange("(h a) -> h a", a=1)).then_inc(taps_in, 16)
            sp.wait_ge(pad_zero, 1)
            sp.dma_start(kp[:, P - 1:P - 1 + D], taps).then_inc(taps_in, 16)
            sp.wait_ge(pad_ready, 1)
            sp.dma_start(kpad, kp[:]).then_inc(pad_out, 16)
            sp.wait_ge(pad_out, 16)

            def load(h, par, first):
                at, row = h * KPAD, h * (P * LB * B * CE)
                if not first:
                    at, row, n = sp.snap(at), sp.snap(row), sp.snap(h + 1)
                    sp.wait_ge(kv_ready, n)
                    sp.wait_ge(conv_done, n)
                sp.dma_start(toe[:, par], bass.AP(tensor=kpad.tensor, offset=at, ap=[[1, P], [1, D]]))\
                    .then_inc(head_in[par], 16)
                sp.dma_start(cc[:, par], bass.AP(tensor=ctx_rev.tensor, offset=row,
                                                 ap=[[LB * B * CE, P], [1, LB * B * CE]])).then_inc(head_in[par], 16)

            load(0, 0, True)
            load(1, 1, True)
            with sp.Fori(1, SH // 2) as i:
                load(2 * i, 0, False)
                load(2 * i + 1, 1, False)

        @block.gpsimd
        def _(pool):
            pool.sem_inc(kv_ready, 2)
            nc.gpsimd.memset(kp[:], 0.0).then_inc(pad_zero, 1)

            def multiply(i, par):
                h = 2 * i + par
                pool.wait_ge(head_in[par], 32 * i + 32)
                pool.wait_ge(conv_done, h + 1)
                c = cc[:, par]
                nc.gpsimd.tensor_tensor(
                    view(kv[:, par], 0, [[ND * CH, LB * B], [CH, ND], [1, CH]]),
                    view(c, 0, [[CE, LB * B], [0, ND], [1, CH]]),
                    view(c, 0, [[CE, LB * B], [1, ND], [1, CH]]), ALU.mult).then_inc(kv_ready, 1)

            with pool.Fori(0, SH // 2) as i:
                multiply(i, 0)
                multiply(i, 1)

        @block.scalar
        def _(act):
            act.sem_inc(even_copied, 1)
            act.sem_inc(ye_ready, 2)
            act.wait_ge(var_ready, 1)
            nc.scalar.activation(rstd[:], rstd[:], ACT.Sqrt).then_inc(std_ready, 1)
            with act.Fori(0, B) as b:
                act.wait_ge(xt_done, 2 * b + 1)
                nc.scalar.activation(q_tile(qe, b, 0, 0), ps_tile(ps, 0), ACT.Copy)
                nc.scalar.activation(q_tile(qe, b, 0, CH), ps_tile(ps, 0), ACT.Copy).then_inc(even_copied, 1)

            def evacuate(h, par):
                act.wait_ge(conv_done, h + 3)
                act.wait_ge(prod_ready, h + 1)
                y = view(ps[:], 4 * par * 512, [[512, LB], [CH, B * ND], [1, CH]])
                for copy in range(2):
                    ins = nc.scalar.activation(
                        view(ye[:, par], copy * CH, [[B * ND * QE, LB], [QE, B * ND], [1, CH]]), y, ACT.Copy)
                ins.then_inc(ye_ready, 1)

            with act.Fori(0, SH // 2) as i:
                evacuate(2 * i, 0)
                evacuate(2 * i + 1, 1)

        @block.tensor
        def _(pe):
            ident = cst[:, C_ID:C_ID + P]
            pe.sem_inc(conv_done, 2)
            with pe.Fori(0, B) as b:
                for t in range(TPB):
                    pe.wait_ge(xn_ready, 2 * b + t + 1)
                    pe.wait_ge((even_copied, odd_copied)[t], b + 1)
                    for k in range(KD):
                        last = nc.tensor.transpose(ps[:, t, k * P:(k + 1) * P], xn[:, t, k * P:(k + 1) * P], ident)
                    last.then_inc(xt_done, 1)

            def convolve(h, i, par):
                pe.wait_ge(head_in[par], 32 * i + 32)
                pe.wait_ge(kv_ready, h + 3)
                pe.wait_ge(ye_ready, h + 1)
                for l in range(LB):
                    for m in range(l + 1):
                        last = nc.tensor.matmul(ps[:, 4 * par + l, 0:NCOL], toe[:, par, (l - m) * P:(l - m + 1) * P],
                                                kv[:, par, m * NCOL:(m + 1) * NCOL],
                                                start=(m == 0), stop=(m == l))
                last.then_inc(conv_done, 1)

            pe.wait_ge(even_copied, B + 1)
            pe.wait_ge(odd_copied, B + 1)
            with pe.Fori(0, SH // 2) as i:
                convolve(2 * i, i, 0)
                convolve(2 * i + 1, i, 1)

        @block.vector
        def _(dve):
            dve.sem_inc(odd_copied, 1)
            dve.sem_inc(prod_ready, 2)
            dve.wait_ge(taps_in, 32)
            nc.vector.tensor_tensor(kp[:, P - 1:P], kp[:, P - 1:P], dd[:], ALU.add).then_inc(pad_ready, 1)
            steps = Steps(dve, dve_step)
            for t in range(NT):
                nc.vector.bn_aggr(mv[:, t], stats1[:, t]).then_inc(aggr, 1)
            dve.wait_ge(aggr, NT)
            nc.vector.tensor_scalar(rstd[:], mv[:, :, 1], EPS, None, ALU.add).then_inc(var_ready, 1)
            dve.wait_ge(std_ready, 1)
            steps.do(nc.vector.reciprocal(rstd[:], rstd[:]))

            def normalise(b, t, first):
                if not first:
                    dve.wait_ge(xt_done, 2 * b + t - 1)
                i = 2 * b + t
                nc.vector.tensor_scalar(xn[:, t], xs[:, i], mv[:, i, 0:1], rstd[:, bass.ds(i, 1)],
                                        ALU.subtract, ALU.mult).then_inc(xn_ready, 1)

            def copy_odd(b):
                dve.wait_ge(xt_done, 2 * b + 2)
                nc.vector.tensor_copy(q_tile(qe, b, 1, 0), ps_tile(ps, 1))
                nc.vector.tensor_copy(q_tile(qe, b, 1, CH), ps_tile(ps, 1)).then_inc(odd_copied, 1)

            normalise(0, 0, True)
            normalise(0, 1, True)
            with dve.Fori(0, B - 1) as b:
                normalise(b + 1, 0, False)
                copy_odd(b)
                normalise(b + 1, 1, False)
            copy_odd(B - 1)
            dve.wait_ge(even_copied, B + 1)
            dve.wait_ge(odd_copied, B + 1)

            def contract(h, par):
                dve.wait_ge(ye_ready, h + 3)
                q = qe[:]
                y = ye[:, par]
                o = prod[:]
                lb_q, lb_y, lb_o = [SH * QE, LB * B], [ND * QE, LB * B], [CH * CH, LB * B]
                nc.vector.tensor_tensor(view(o, 0, [lb_o, [CH, ND], [1, CH]]),
                                        view(y, 0, [lb_y, [QE, ND], [1, CH]]),
                                        view(q, h * QE, [lb_q, [1, ND], [1, CH]]), ALU.mult)
                nc.vector.tensor_tensor(view(o, ND * CH, [lb_o, [CH, CH - ND], [1, CH]]),
                                        view(y, 3 * (QE - 1) + CH, [lb_y, [1 - QE, CH - ND], [1, CH]]),
                                        view(q, h * QE + CH - 3, [lb_q, [1, CH - ND], [1, CH]]), ALU.mult)\
                    .then_inc(prod_ready, 1)
                dve.wait_ge(prod_ready, h + 3)
                nc.vector.tensor_reduce(view(res[:], h * CH, [[S, LB * B], [1, CH]]),
                                        view(o, 0, [lb_o, [1, CH], [CH, CH]]), AX_X, ALU.add).then_inc(res_ready, 1)
                dve.wait_ge(res_ready, h + 1)

            with dve.Fori(0, SH // 2) as i:
                contract(2 * i, 0)
                contract(2 * i + 1, 1)


def q_tile(qe, b, t, at):
    return view(qe[:], b * (SH * QE) + t * (SH // 2) * QE + at, [[B * SH * QE, LB], [QE, SH // 2], [1, CH]])


def ps_tile(ps, t):
    return view(ps[:], t * 512, [[P, LB], [CH, SH // 2], [1, CH]])


def route(nc, xs, cst, res, w_sb, b2_sb, w_in, wr, br, w1, w2, b2, b1, b1_sb, xnd, acc, tabs):
    gidx, sidx, wt, eid, tstart_i = tabs
    with ExitStack() as ctx:
        def sb(name, shape, dt=F32):
            return ctx.enter_context(nc.sbuf_tensor(name, shape, dt))

        def psum(name, shape):
            return ctx.enter_context(nc.psum_tensor(name, shape, F32))

        def sem(name):
            return ctx.enter_context(nc.semaphore(name))

        TE = NT * E
        stats = sb("stats_c", [P, NT, 6])
        mv = sb("mv_c", [P, NT, 2])
        rstd = sb("rstd_c", [P, NT])
        wr_sb = sb("wr_sb", [P, KD * E])
        br_sb = sb("br_sb", [P, E])
        xn = sb("xn_c", [P, TPB, D])
        xT = sb("xT_c", [P, TPB, KD * P])
        prob = sb("prob", [P, NT, E])
        ex = sb("ex", [P, NT, E])
        rank = sb("rank", [P, NT, E])
        sel = sb("sel", [P, NT, E])
        ew = sb("ew", [P, NT, E])
        slot = sb("slot", [P, NT, E])
        before = sb("before", [P, NT, E])
        col = sb("col", [P, 4, NT])
        cnt = sb("cnt", [P, 8, E])
        slot3 = sb("slot3", [P, TOPK, NT])
        slot3_i = sb("slot3_i", [P, 3, TOPK * NT], I32)
        slot3_f = sb("slot3_f", [P, 2, TOPK * NT])
        tile_f = sb("tile_f", [P, 3, NTILE])
        ONE_HOT = NT * (P + NTILE)
        work = sb("work", [P, 2 * ONE_HOT])

        ps_r = psum("ps_r", [P, 2, 512])
        ps_x = psum("ps_x", [P, 2, 512])
        ps_l = psum("ps_l", [P, 2, 512])
        ps_c = psum("ps_c", [P, 512])
        ps_m = psum("ps_m", [P, 512])

        small_in, zeroed, acc_out = sem("small_in"), sem("zeroed"), sem("acc_out")
        rt_done = sem("rt_done")
        x2_ready = sem("x2_ready")
        aggr = sem("aggr_c")
        var_ready, std_ready = sem("var_ready_c"), sem("std_ready_c")
        dve_step = sem("dve_step_c")
        xn_ready = sem("xn_ready_c")
        xt_done = sem("xt_done_c")
        xt_evac = sem("xt_evac_c")
        logit_done = sem("logit_done")
        logit_read = sem("logit_read")
        xn_out = [sem("xn_out0"), sem("xn_out1")]
        exp_in, exp_out = sem("exp_in"), sem("exp_out")
        sel_ready, counted = sem("sel_ready"), sem("counted")
        hot_ready, hot_used = sem("hot_ready"), sem("hot_used")

        block = ctx.enter_context(nc.Block())

        @block.sync
        def _(sp):
            sp.dma_start(wr_sb[:].rearrange("p (k e) -> p k e", k=KD), wr.rearrange("(k p) e -> p k e", p=P))\
                .then_inc(small_in, 16)
            sp.dma_start(br_sb[:], br.partition_broadcast(P)).then_inc(small_in, 16)
            sp.dma_start(b1_sb[:], b1).then_inc(small_in, 16)
            sp.sem_inc(w_in[1], 48)
            for e in range(2):
                load_expert(sp, w_sb, b2_sb, w_in, w1, w2, b2, e, e)

            def store(b, t):
                at = sp.snap((2 * b + t) * (P * D))
                n = sp.snap(2 * b + t + 1)
                sp.wait_ge(xn_ready, n)
                sp.dma_start(bass.AP(tensor=xnd.tensor, offset=at, ap=[[D, P], [1, D]]), xn[:, t])\
                    .then_inc(xn_out[t], 16)

            with sp.Fori(0, B) as b:
                store(b, 0)
                store(b, 1)
            sp.wait_ge(xn_out[0], 16 * B)
            sp.wait_ge(xn_out[1], 16 * B)
            sp.wait_ge(small_in, 48)

        @block.gpsimd
        def _(pool):
            nc.gpsimd.memset(work[:, 0:D], 0.0).then_inc(zeroed, 1)
            pool.wait_ge(zeroed, 1)
            pool.dma_start(acc.rearrange("(t p) d -> p t d", p=P), view(work[:], 0, [[0, NT + 1], [1, D]]))\
                .then_inc(acc_out, 16)
            pool.wait_ge(acc_out, 16)

        @block.scalar
        def _(act):
            act.sem_inc(xt_evac, 2)
            act.wait_ge(var_ready, 1)
            nc.scalar.activation(rstd[:], rstd[:], ACT.Sqrt).then_inc(std_ready, 1)

            def evacuate(b, t):
                act.wait_ge(xt_done, 2 * b + t + 1)
                act.wait_ge(logit_done, 2 * b + t + 1)
                nc.scalar.activation(xT[:, t], ps_x[:, t], ACT.Copy).then_inc(xt_evac, 1)

            with act.Fori(0, B) as b:
                evacuate(b, 0)
                evacuate(b, 1)
            for n in range(2):
                act.wait_ge(exp_in, n + 1)
                nc.scalar.activation(ex[:], ex[:], ACT.Exp).then_inc(exp_out, 1)

        @block.tensor
        def _(pe):
            ident = cst[:, C_ID:C_ID + P]
            pe.sem_inc(logit_done, 2)
            for i in range(NT):
                if i > 1:
                    pe.wait_ge(x2_ready, i - 1)
                for l in range(LB):
                    at = (l * B + i // TPB) * S + i % TPB * P
                    last = nc.tensor.transpose(ps_r[:, i % 2, l * P:(l + 1) * P], res[:, at:at + P], ident)
                last.then_inc(rt_done, 1)
            pe.wait_ge(small_in, 48)

            def transposes(b, t):
                pe.wait_ge(xn_ready, 2 * b + t + 1)
                pe.wait_ge(xt_evac, 2 * b + t + 1)
                for k in range(KD):
                    last = nc.tensor.transpose(ps_x[:, t, k * P:(k + 1) * P], xn[:, t, k * P:(k + 1) * P], ident)
                last.then_inc(xt_done, 1)

            def logits(b, t):
                pe.wait_ge(xt_evac, 2 * b + t + 3)
                pe.wait_ge(logit_read, 2 * b + t + 1)
                for k in range(KD):
                    last = nc.tensor.matmul(ps_l[:, t, 0:E], xT[:, t, k * P:(k + 1) * P],
                                            wr_sb[:, k * E:(k + 1) * E], start=(k == 0), stop=(k == KD - 1))
                last.then_inc(logit_done, 1)

            with pe.Fori(0, B) as b:
                transposes(b, 0)
                transposes(b, 1)
                logits(b, 0)
                logits(b, 1)

            pe.wait_ge(sel_ready, 1)
            flat = sel[:].rearrange("p t e -> p (t e)")
            nc.tensor.matmul(ps_c[:, 0:TE], cst[:, C_UP:C_UP + P], flat, start=True, stop=True)
            nc.tensor.matmul(ps_m[:, 0:TE], cst[:, C_ONE:C_ONE + P], flat, start=True, stop=True)
            nc.tensor.matmul(ps_m[:, TE:2 * TE], cst[:, C_ONE:C_ONE + P], ew[:].rearrange("p t e -> p (t e)"),
                             start=True, stop=True).then_inc(counted, 1)
            for k in range(TOPK):
                pe.wait_ge(hot_ready, k + 1)
                oc, oa = one_hots(work, k, ONE_HOT)
                for t in range(NT):
                    last = nc.tensor.matmul(ps_r[:, 0, 0:NTILE], oc[:, t * P:(t + 1) * P],
                                            oa[:, t * NTILE:(t + 1) * NTILE], start=(k == 0 and t == 0),
                                            stop=(k == TOPK - 1 and t == NT - 1))
                last.then_inc(hot_used, 1)

        @block.vector
        def _(dve):
            dve.sem_inc(logit_read, 2)
            v = nc.vector
            steps = Steps(dve, dve_step)
            do = steps.do

            def add_conv(b, t):
                i = 2 * b + t
                dve.wait_ge(rt_done, i + 1)
                v.tensor_tensor(xs[:, i], xs[:, i], ps_r[:, t], ALU.add).then_inc(x2_ready, 1)
                dve.wait_ge(x2_ready, i + 1)
                v.bn_stats(stats[:, i], xs[:, i]).then_inc(aggr, 1)

            with dve.Fori(0, B) as b:
                add_conv(b, 0)
                add_conv(b, 1)
            dve.wait_ge(aggr, NT)
            for t in range(NT):
                v.bn_aggr(mv[:, t], stats[:, t]).then_inc(aggr, 1)
            dve.wait_ge(aggr, 2 * NT)
            v.tensor_scalar(rstd[:], mv[:, :, 1], EPS, None, ALU.add).then_inc(var_ready, 1)
            dve.wait_ge(std_ready, 1)
            do(v.reciprocal(rstd[:], rstd[:]))

            def normalise(b, t, first):
                if not first:
                    dve.wait_ge(xt_done, 2 * b + t - 1)
                    dve.wait_ge(xn_out[t], 16 * b)
                i = 2 * b + t
                v.tensor_scalar(xn[:, t], xs[:, i], mv[:, i, 0:1], rstd[:, bass.ds(i, 1)],
                                ALU.subtract, ALU.mult).then_inc(xn_ready, 1)

            def take_logits(b, t):
                dve.wait_ge(logit_done, 2 * b + t + 3)
                v.tensor_tensor(prob[:, 2 * b + t], ps_l[:, t, 0:E], br_sb[:], ALU.add).then_inc(logit_read, 1)

            normalise(0, 0, True)
            normalise(0, 1, True)
            dve.wait_ge(small_in, 48)
            with dve.Fori(0, B - 1) as b:
                normalise(b + 1, 0, False)
                normalise(b + 1, 1, False)
                take_logits(b, 0)
                take_logits(b, 1)
            take_logits(B - 1, 0)
            take_logits(B - 1, 1)
            dve.wait_ge(logit_read, NT + 2)

            mx, den = col[:, 0], col[:, 1]
            do(v.tensor_reduce(mx, prob[:], AX_X, ALU.max))
            v.tensor_tensor(ex[:], prob[:], bc(mx, E), ALU.subtract).then_inc(exp_in, 1)
            dve.wait_ge(exp_out, 1)
            do(v.tensor_reduce(den, ex[:], AX_X, ALU.add))
            do(v.reciprocal(den, den))
            do(v.tensor_tensor(prob[:], ex[:], bc(den, E), ALU.mult))
            gt = view(work[:], 0, [[E * E, NT], [E, E], [1, E]])
            eq = view(work[:], NT * E * E, [[E * E, NT], [E, E], [1, E]])
            other = view(prob[:], 0, [[E, NT], [0, E], [1, E]])
            own = view(prob[:], 0, [[E, NT], [1, E], [0, E]])
            low = view(cst[:], C_LOW, [[0, NT], [E, E], [1, E]])
            dve.wait_ge(acc_out, 16)
            v.tensor_tensor(gt, other, own, ALU.is_gt)
            do(v.tensor_tensor(eq, other, own, ALU.is_equal))
            do(v.tensor_tensor(eq, eq, low, ALU.mult))
            do(v.tensor_tensor(gt, gt, eq, ALU.add))
            do(v.tensor_reduce(rank[:], gt, AX_X, ALU.add))
            do(v.tensor_scalar(sel[:], rank[:], float(TOPK), None, ALU.is_lt))
            do(v.tensor_reduce(mx, prob[:], AX_X, ALU.max))
            v.tensor_tensor(ex[:], prob[:], bc(mx, E), ALU.subtract).then_inc(exp_in, 1)
            dve.wait_ge(exp_out, 2)
            do(v.tensor_tensor(ex[:], ex[:], sel[:], ALU.mult))
            do(v.tensor_reduce(den, ex[:], AX_X, ALU.add))
            do(v.reciprocal(den, den))
            v.tensor_tensor(ew[:], ex[:], bc(den, E), ALU.mult).then_inc(sel_ready, 1)
            dve.wait_ge(counted, 1)

            count, inv, weight, ntile, tstart, tend = (cnt[:, i] for i in range(6))
            do(v.memset(before[:, 0], 0.0))
            for t in range(1, NT):
                do(v.tensor_tensor(before[:, t], before[:, t - 1], ps_m[:, (t - 1) * E:t * E], ALU.add))
            do(v.tensor_tensor(count, before[:, NT - 1], ps_m[:, (NT - 1) * E:NT * E], ALU.add))
            v.tensor_reduce(weight, view(ps_m[:], TE, [[1, E], [E, NT]]), AX_X, ALU.add)
            do(v.tensor_scalar(inv, count, 1.0, None, ALU.max))
            do(v.reciprocal(inv, inv))
            do(v.tensor_tensor(weight, weight, inv, ALU.mult))
            full = view(work[:], 0, [[NT, E], [1, NT]])
            do(v.tensor_scalar(inv, count, 1.0 / P, None, ALU.mult))
            do(v.tensor_tensor(full, bc(inv, NT), view(cst[:], C_IOTA, [[0, E], [1, NT]]), ALU.is_gt))
            do(v.tensor_reduce(ntile, full, AX_X, ALU.add))
            pair = view(work[:], 0, [[E, E], [1, E]])
            do(v.tensor_tensor(pair, view(cst[:], C_LOW, [[E, E], [1, E]]), view(ntile, 0, [[0, E], [1, E]]), ALU.mult))
            do(v.tensor_reduce(tstart, pair, AX_X, ALU.add))
            v.tensor_copy(tstart_i[:], tstart[0:1])
            do(v.tensor_tensor(tend, tstart, ntile, ALU.add))
            tile_e = view(work[:], 0, [[E, NTILE], [1, E]])
            expert, is_e, first = tile_f[:, 0], tile_f[:, 1], tile_f[:, 2]
            do(v.tensor_tensor(tile_e, view(cst[:], C_IOTA, [[1, NTILE], [0, E]]), view(tend, 0, [[0, NTILE], [1, E]]),
                               ALU.is_ge))
            do(v.tensor_reduce(expert, tile_e, AX_X, ALU.add))
            do(v.tensor_scalar(expert, expert, float(E - 1), None, ALU.min))
            v.tensor_copy(eid[:], expert[0:1])
            do(v.tensor_tensor(tile_e, view(cst[:], C_IOTA, [[0, NTILE], [1, E]]), bc(expert, E), ALU.is_equal))
            do(v.tensor_tensor(tile_e, tile_e, view(weight, 0, [[0, NTILE], [1, E]]), ALU.mult))
            do(v.tensor_reduce(wt[:], tile_e, AX_X, ALU.add))
            do(v.tensor_tensor(slot[:], before[:], ps_c[:, 0:TE].rearrange("p (t e) -> p t e", e=E), ALU.add))
            do(v.tensor_scalar(inv, tstart, float(P), None, ALU.mult))
            do(v.tensor_tensor(slot[:], slot[:], view(inv, 0, [[0, NT], [1, E]]), ALU.add))
            for k in range(TOPK):
                do(v.scalar_tensor_tensor(ex[:], rank[:], float(k), slot[:], ALU.is_equal, ALU.mult))
                do(v.tensor_reduce(slot3[:, k], ex[:], AX_X, ALU.add))
            s_all, s_tile, s_place = (slot3_i[:, i] for i in range(3))
            f_tile, f_place = slot3_f[:, 0], slot3_f[:, 1]
            do(v.tensor_copy(s_all, slot3[:].rearrange("p k t -> p (k t)")))
            v.tensor_single_scalar(s_tile, s_all, 7, ALU.arith_shift_right)
            do(v.tensor_single_scalar(s_place, s_all, P - 1, ALU.bitwise_and))
            v.tensor_copy(f_tile, s_tile)
            do(v.tensor_copy(f_place, s_place))
            for k in range(TOPK):
                if k > 1:
                    dve.wait_ge(hot_used, k - 1)
                oc, oa = one_hots(work, k, ONE_HOT)
                oc = oc.rearrange("p (t c) -> p t c", t=NT)
                oa = oa.rearrange("p (t c) -> p t c", t=NT)
                v.tensor_tensor(oc, view(cst[:], C_IOTA, [[0, NT], [1, P]]),
                                bc(f_place[:, k * NT:(k + 1) * NT], P), ALU.is_equal)
                do(v.tensor_tensor(oa, view(cst[:], C_IOTA, [[0, NT], [1, NTILE]]),
                                   bc(f_tile[:, k * NT:(k + 1) * NT], NTILE), ALU.is_equal))
                v.tensor_tensor(oa, oa, bc(cst[:, C_TOK:C_TOK + NT], NTILE), ALU.mult).then_inc(hot_ready, 1)
            dve.wait_ge(hot_used, TOPK)
            m = ps_r[:, 0, 0:NTILE]
            used, tok = is_e, first
            trash = cst[:, C_TRASH:C_TRASH + 1]
            v.tensor_scalar(used, m, 0.5, None, ALU.is_gt)
            do(v.tensor_scalar(tok, m, -1.0, 0.0, ALU.add, ALU.max))
            v.tensor_copy(gidx[:], tok)
            do(v.tensor_scalar(expert, tok, trash, None, ALU.subtract))
            do(v.tensor_tensor(expert, expert, used, ALU.mult))
            do(v.tensor_scalar(expert, expert, trash, None, ALU.add))
            v.tensor_copy(sidx[:], expert)


def one_hots(work, k, size):
    at = (k % 2) * size
    return work[:, at:at + NT * P], work[:, at + NT * P:at + size]


def load_expert(eng, w_sb, b2_sb, w_in, w1, w2, b2, e, par):
    cols = KD * FF
    w1_at, w2_at, b2_at = e * (D * FF), e * (FF * D), e * D
    if not isinstance(e, int):
        w1_at, w2_at, b2_at = eng.snap(w1_at), eng.snap(w2_at), eng.snap(b2_at)

    def go():
        eng.dma_start(w_sb[:, par, 0:cols].rearrange("p (k n) -> p k n", k=KD),
                      bass.AP(tensor=w1.tensor, offset=w1_at, ap=[[FF, P], [P * FF, KD], [1, FF]]))\
            .then_inc(w_in[par], 16)
        eng.dma_start(w_sb[:, par, cols:].rearrange("p (k n) -> p k n", k=KF),
                      bass.AP(tensor=w2.tensor, offset=w2_at, ap=[[D, P], [P * D, KF], [1, D]]))\
            .then_inc(w_in[par], 16)
        eng.dma_start(b2_sb[:, par], bass.AP(tensor=b2.tensor, offset=b2_at, ap=[[0, P], [1, D]]))\
            .then_inc(w_in[par], 16)

    if isinstance(e, int):
        go()
    return go


def experts(nc, cst, w_sb, b2_sb, w_in, w1, w2, b2, b1_sb, xnd, acc, tabs):
    gidx, sidx, wt, eid, tstart_i = tabs
    WS = KD * FF + KF * D
    with ExitStack() as ctx:
        def sb(name, shape, dt=F32):
            return ctx.enter_context(nc.sbuf_tensor(name, shape, dt))

        def psum(name, shape):
            return ctx.enter_context(nc.psum_tensor(name, shape, F32))

        def sem(name):
            return ctx.enter_context(nc.semaphore(name))

        gi = sb("gi", [P, 2], U32)
        si = sb("si", [P, 2], U32)
        tick = sb("tick", [P, 1])
        xg = sb("xg", [P, 2, D])
        xT = sb("xT_d", [P, KD * P])
        h = sb("h", [P, 2, FF])
        hT = sb("hT", [P, FF])
        hr = sb("hr", [P, FF])
        yb = sb("yb", [P, D])
        y = sb("y", [P, 2, D])
        ps_x = psum("ps_xd", [P, 512])
        ps_h = psum("ps_h", [P, 3, 512])
        ps_t = psum("ps_td", [P, 3, 512])
        ps_y = psum("ps_y", [P, 512])
        CHUNKS = [(0, 512), (512, 1024), (1024, FF)]

        gi_ready, si_ready = sem("gi_ready"), sem("si_ready")
        g_in = [sem("g_in0"), sem("g_in1")]
        x_done = sem("x_done")
        x_evac = sem("x_evac")
        h_done = sem("h_done")
        h_evac = sem("h_evac")
        t_done = sem("t_done")
        hb_done = sem("hb_done")
        relu_done = sem("relu_done")
        y_done = sem("y_done")
        y_read = sem("y_read")
        y_ready = sem("y_ready")
        added = sem("added")

        block = ctx.enter_context(nc.Block())

        @block.sync
        def _(sp):
            def load(e, par):
                go = load_expert(sp, w_sb, b2_sb, w_in, w1, w2, b2, e, par)
                n = sp.snap(sp.value_load(tstart_i[0:1, bass.ds(e - 1, 1)], min_val=0, max_val=NTILE) + 1)
                sp.wait_ge(y_read, n)
                go()

            with sp.Fori(1, E // 2) as i:
                load(2 * i, 0)
                load(2 * i + 1, 1)
            sp.wait_ge(w_in[0], 48 * (E // 2))
            sp.wait_ge(w_in[1], 48 * (E // 2) + 48)

        @block.gpsimd
        def _(pool):
            def gather(i, j, par, first):
                if not first:
                    pool.wait_ge(x_done, i - 1)
                nc.gpsimd.tensor_copy(gi[:, par:par + 1], gidx[:, bass.ds(i, 1)]).then_inc(gi_ready, 1)
                pool.wait_ge(gi_ready, i + 1)
                nc.gpsimd.tensor_tensor(tick[:], wt[:, 0:1], wt[:, 0:1], ALU.add)
                pool.indirect_dma_start(xg[:, par], None, xnd,
                                        bass.IndirectOffsetOnAxis(ap=gi[:, par:par + 1], axis=0))\
                    .then_inc(g_in[par], 16)

            def scatter(i, par):
                nc.gpsimd.tensor_copy(si[:, par:par + 1], sidx[:, bass.ds(i, 1)]).then_inc(si_ready, 1)
                pool.wait_ge(si_ready, i + 1)
                pool.wait_ge(y_ready, i + 1)
                nc.gpsimd.tensor_tensor(tick[:], wt[:, 0:1], wt[:, 0:1], ALU.add)
                pool.indirect_dma_start(acc, bass.IndirectOffsetOnAxis(ap=si[:, par:par + 1], axis=0),
                                        y[:, par], None, compute_op=ALU.add).then_inc(added, 16)
                pool.wait_ge(added, 16 * i + 16)

            gather(0, 0, 0, True)
            gather(1, 0, 1, True)
            with pool.Fori(0, NTILE // 2 - 1) as j:
                for par in range(2):
                    gather(2 * j + par + 2, j + 1, par, False)
                    scatter(2 * j + par, par)
            scatter(NTILE - 2, 0)
            scatter(NTILE - 1, 1)

        @block.scalar
        def _(act):
            act.sem_inc(x_evac, 1)

            def evac_x(i):
                act.wait_ge(x_done, i + 1)
                nc.scalar.activation(xT[:], ps_x[:], ACT.Copy).then_inc(x_evac, 1)

            def evac_h(i, par, c):
                lo, hi = CHUNKS[c]
                act.wait_ge(h_done, 3 * i + c + 1)
                nc.scalar.activation(h[:, par, lo:hi], ps_h[:, c, 0:hi - lo], ACT.Copy).then_inc(h_evac, 1)

            def relu(i):
                act.wait_ge(hb_done, i + 2)
                nc.scalar.activation(hr[:], hT[:], ACT.Relu).then_inc(relu_done, 1)

            def tile(i, par, w1_next, x_next):
                if w1_next:
                    evac_h(i + 1, 1 - par, 0)
                relu(i)
                if w1_next:
                    evac_h(i + 1, 1 - par, 1)
                    evac_h(i + 1, 1 - par, 2)
                if x_next:
                    evac_x(i + 2)

            evac_x(0)
            for c in range(3):
                evac_h(0, 0, c)
            evac_x(1)
            with act.Fori(0, NTILE // 2 - 1) as j:
                tile(2 * j, 0, True, True)
                tile(2 * j + 1, 1, True, True)
            tile(NTILE - 2, 0, True, False)
            tile(NTILE - 1, 1, False, False)

        @block.vector
        def _(dve):
            dve.sem_inc(hb_done, 1)
            dve.sem_inc(y_read, 1)

            def expert_of(i):
                return dve.value_load(eid[0:1, bass.ds(i, 1)], min_val=0, max_val=E - 1)

            def add_b1(i, e):
                dve.wait_ge(t_done, i + 1)
                if not isinstance(i, int) or i:
                    dve.wait_ge(relu_done, i)
                for c, (lo, hi) in enumerate(CHUNKS):
                    n = (hi - lo) // P
                    ins = nc.vector.tensor_tensor(view(hT[:], lo, [[P, n], [1, P]]),
                                                  view(ps_t[:], c * 512, [[P, n], [1, P]]),
                                                  view(b1_sb[:], e * KF + lo // P, [[1, n], [0, P]]), ALU.add)
                ins.then_inc(hb_done, 1)

            def result(i, par, e, first):
                dve.wait_ge(y_done, i + 1)
                b2_of = view(b2_sb[:], (e % 2) * D, [[1, D]])
                nc.vector.tensor_tensor(yb[:], ps_y[:], b2_of, ALU.add).then_inc(y_read, 1)
                dve.wait_ge(y_read, i + 2)
                if not first:
                    dve.wait_ge(added, 16 * i - 16)
                nc.vector.tensor_scalar(y[:, par], yb[:], wt[:, bass.ds(i, 1)], None, ALU.mult)\
                    .then_inc(y_ready, 1)
                dve.wait_ge(y_ready, i + 1)

            def tile(i, par, first=False):
                e = expert_of(i)
                add_b1(i, e)
                result(i, par, e, first)

            tile(0, 0, True)
            tile(1, 1, True)
            with dve.Fori(1, NTILE // 2) as j:
                tile(2 * j, 0)
                tile(2 * j + 1, 1)

        @block.tensor
        def _(pe):
            ident = cst[:, C_ID:C_ID + P]

            def expert_of(i):
                return pe.value_load(eid[0:1, bass.ds(i, 1)], min_val=0, max_val=E - 1)

            def x_t(i, j, par):
                pe.wait_ge(g_in[par], 16 * j + 16)
                pe.wait_ge(x_evac, i + 1)
                for k in range(KD):
                    last = nc.tensor.transpose(ps_x[:, k * P:(k + 1) * P], xg[:, par, k * P:(k + 1) * P], ident)
                last.then_inc(x_done, 1)

            def first_product(i, e, c, first):
                lo, hi = CHUNKS[c]
                if not first:
                    pe.wait_ge(h_evac, 3 * i + c - 2)
                for k in range(KD):
                    rhs = view(w_sb[:], (e % 2) * WS + k * FF + lo, [[1, hi - lo]])
                    last = nc.tensor.matmul(ps_h[:, c, 0:hi - lo], xT[:, k * P:(k + 1) * P], rhs,
                                            start=(k == 0), stop=(k == KD - 1))
                last.then_inc(h_done, 1)

            def start_first(i, e):
                pe.wait_ge(x_evac, i + 2)
                pe.wait_ge(w_in[0], ((e + 2) // 2) * 48)
                pe.wait_ge(w_in[1], ((e + 3) // 2) * 48)

            def h_t(i, par):
                pe.wait_ge(h_evac, 3 * i + 3)
                pe.wait_ge(hb_done, i + 1)
                for k in range(KF):
                    last = nc.tensor.transpose(ps_t[:, k // 4, (k % 4) * P:(k % 4 + 1) * P],
                                               h[:, par, k * P:(k + 1) * P], ident)
                last.then_inc(t_done, 1)

            def second_product(i, e):
                pe.wait_ge(relu_done, i + 1)
                pe.wait_ge(y_read, i + 1)
                for k in range(KF):
                    rhs = view(w_sb[:], (e % 2) * WS + KD * FF + k * D, [[1, D]])
                    last = nc.tensor.matmul(ps_y[:], hr[:, k * P:(k + 1) * P], rhs,
                                            start=(k == 0), stop=(k == KF - 1))
                last.then_inc(y_done, 1)

            def tile(i, j, par, w1_next, x_next):
                if w1_next:
                    e = expert_of(i + 1)
                    start_first(i + 1, e)
                    first_product(i + 1, e, 0, False)
                h_t(i, par)
                if w1_next:
                    first_product(i + 1, e, 1, False)
                    first_product(i + 1, e, 2, False)
                if x_next:
                    x_t(i + 2, j + 1, par)
                second_product(i, expert_of(i))

            x_t(0, 0, 0)
            e0 = expert_of(0)
            start_first(0, e0)
            for c in range(3):
                first_product(0, e0, c, True)
            x_t(1, 0, 1)
            with pe.Fori(0, NTILE // 2 - 1) as j:
                tile(2 * j, j, 0, True, True)
                tile(2 * j + 1, j, 1, True, True)
            tile(NTILE - 2, None, 0, True, False)
            tile(NTILE - 1, None, 1, False, False)


def finish(nc, xs, cst, res, acc, wp1, bp1, wp2, bp2, out):
    PH = wp1.shape[1]
    KP = PH // P
    with ExitStack() as ctx:
        def sb(name, shape, dt=F32):
            return ctx.enter_context(nc.sbuf_tensor(name, shape, dt))

        def sem(name):
            return ctx.enter_context(nc.semaphore(name))

        wp1_sb = sb("wp1_sb", [P, KD, PH])
        bp1_sb = sb("bp1_sb", [P, KP])
        wp2_sb = sb("wp2_sb", [P, KP])
        wp2_b = sb("wp2_b", [P, KP, P])
        bp2_sb = sb("bp2_sb", [P, 1])
        pooled = sb("pooled", [P, KD * B])
        hid = sb("hid", [P, KP, B])
        z = sb("z", [P, B])
        ps_pool = ctx.enter_context(nc.psum_tensor("ps_pool", [P, 512], F32))
        ps_hid = ctx.enter_context(nc.psum_tensor("ps_hid", [P, 512], F32))
        ps_z = ctx.enter_context(nc.psum_tensor("ps_z", [P, 512], F32))
        small_in = sem("small_in_e")
        o_in = [sem(f"o_in{i}") for i in range(4)]
        pooled_done, pooled_ready, wide, hid_done, hid_ready, z_done, z_ready, e_ready, step, gated, stored = (
            sem(n) for n in ("pooled_done", "pooled_ready", "wide", "hid_done", "hid_ready", "z_done", "z_ready",
                             "e_ready", "step_e", "gated", "stored"))
        o = res[:].rearrange("p (t d) -> p t d", t=NT)
        block = ctx.enter_context(nc.Block())

        @block.sync
        def _(sp):
            src = acc.rearrange("(t p) d -> p t d", p=P)
            for i in range(4):
                sp.dma_start(o[:, 4 * i:4 * i + 4], src[:, 4 * i:4 * i + 4]).then_inc(o_in[i], 16)
            dst = out.rearrange("b (t p) d -> p (b t) d", p=P)
            for i in range(B):
                sp.wait_ge(gated, 2 * i + 2)
                sp.dma_start(dst[:, 2 * i:2 * i + 2], o[:, 2 * i:2 * i + 2]).then_inc(stored, 16)
            sp.wait_ge(stored, 16 * B)

        @block.scalar
        def _(act):
            act.dma_start(wp1_sb[:], wp1.rearrange("(k p) n -> p k n", p=P)).then_inc(small_in, 16)
            act.dma_start(bp1_sb[:], bp1).then_inc(small_in, 16)
            act.dma_start(wp2_sb[:], wp2).then_inc(small_in, 16)
            act.dma_start(bp2_sb[:], bp2.partition_broadcast(P)).then_inc(small_in, 16)
            act.wait_ge(small_in, 64)
            act.wait_ge(pooled_done, 1)
            nc.scalar.activation(pooled[:], ps_pool[:, 0:KD * B], ACT.Copy, scale=1.0 / S).then_inc(pooled_ready, 1)
            act.wait_ge(hid_done, 1)
            for c in range(KP):
                last = nc.scalar.activation(hid[:, c], ps_hid[:, c * B:(c + 1) * B], ACT.Relu, bias=bp1_sb[:, c:c + 1])
            last.then_inc(hid_ready, 1)
            act.wait_ge(z_ready, 1)
            nc.scalar.activation(z[:], z[:], ACT.Exp, scale=-1.0).then_inc(e_ready, 1)

        @block.tensor
        def _(pe):
            for b in range(B):
                if b % 2 == 0:
                    pe.wait_ge(o_in[b // 2], 16)
                for k in range(KD):
                    for t in range(TPB):
                        last = nc.tensor.matmul(ps_pool[:, k * B + b:k * B + b + 1],
                                                o[:, 2 * b + t, k * P:(k + 1) * P], cst[:, C_ONE:C_ONE + 1],
                                                start=(t == 0), stop=(t == TPB - 1))
            last.then_inc(pooled_done, 1)
            pe.wait_ge(small_in, 64)
            pe.wait_ge(pooled_ready, 1)
            for c in range(KP):
                for k in range(KD):
                    last = nc.tensor.matmul(ps_hid[:, c * B:(c + 1) * B], wp1_sb[:, k, c * P:(c + 1) * P],
                                            pooled[:, k * B:(k + 1) * B], start=(k == 0), stop=(k == KD - 1))
            last.then_inc(hid_done, 1)
            pe.wait_ge(wide, 1)
            pe.wait_ge(hid_ready, 1)
            for c in range(KP):
                last = nc.tensor.matmul(ps_z[:, 0:B], wp2_b[:, c], hid[:, c], start=(c == 0), stop=(c == KP - 1))
            last.then_inc(z_done, 1)

        @block.vector
        def _(dve):
            do = Steps(dve, step).do
            dve.wait_ge(small_in, 64)
            nc.vector.tensor_copy(wp2_b[:], bc(wp2_sb[:], P)).then_inc(wide, 1)
            dve.wait_ge(z_done, 1)
            nc.vector.tensor_scalar(z[:], ps_z[:, 0:B], bp2_sb[:], None, ALU.add).then_inc(z_ready, 1)
            dve.wait_ge(e_ready, 1)
            do(nc.vector.tensor_scalar(z[:], z[:], 1.0, None, ALU.add))
            do(nc.vector.reciprocal(z[:], z[:]))
            do(nc.vector.tensor_scalar(z[:], z[:], 0.7, -0.8, ALU.is_gt, ALU.mult))
            do(nc.vector.tensor_scalar(z[:], z[:], 1.0, None, ALU.add))
            for i in range(4):
                dve.wait_ge(o_in[i], 16)
            with dve.Fori(0, B) as b:
                for t in range(TPB):
                    nc.vector.scalar_tensor_tensor(o[:, 2 * b + t], o[:, 2 * b + t], z[:, bass.ds(b, 1)],
                                                   xs[:, 2 * b + t], ALU.mult, ALU.add).then_inc(gated, 1)


def decoder_layer(nc, out, **a):
    with ExitStack() as ctx:
        def sb(name, shape, dt=F32):
            return ctx.enter_context(nc.sbuf_tensor(name, shape, dt))

        xs = sb("xs", [P, NT, D])
        cst = sb("cst", [P, NCONST])
        stats1 = sb("stats1", [P, NT, 6])
        res = sb("res", [P, LB * B * S])
        tabs = (sb("gidx", [P, NTILE], U32), sb("sidx", [P, NTILE], U32), sb("wt", [P, NTILE]),
                sb("eid", [1, NTILE], I32), sb("tstart_i", [1, E], I32))
        kpad = nc.dram_tensor("kpad", (SH, KPAD), F32, kind="Internal").ap()
        xnd = nc.dram_tensor("xnd", (NT * P, D), F32, kind="Internal").ap()
        acc = nc.dram_tensor("acc", (NT * P + P, D), F32, kind="Internal").ap()
        w_in = [ctx.enter_context(nc.semaphore(f"w_in{i}")) for i in range(2)]
        attention(nc, xs, cst, a["x"], a["L0_attn_Wq"], a["L0_attn_Wk"], a["L0_attn_Wv"], a["L0_attn_Wo"],
                  a["L0_attn_bq"], a["L0_attn_bk"], a["L0_attn_bv"], a["L0_attn_bo"], a["consts"], stats1)
        convolution(nc, xs, cst, stats1, res, a["ctx_rev"], a["L0_xattn_ssm_kernel"], a["L0_xattn_D"], kpad)
        with ExitStack() as late:
            w_sb = late.enter_context(nc.sbuf_tensor("w_sb", [P, 2, KD * FF + KF * D], F32))
            b2_sb = late.enter_context(nc.sbuf_tensor("b2_sb", [P, 2, D], F32))
            b1_sb = late.enter_context(nc.sbuf_tensor("b1_sb", [P, E * KF], F32))
            w1, w2, b2 = a["L0_ffn_w1"], a["L0_ffn_w2"], a["L0_ffn_b2"]
            route(nc, xs, cst, res, w_sb, b2_sb, w_in, a["L0_ffn_Wr"], a["L0_ffn_br"], w1, w2, b2,
                  a["L0_ffn_b1"], b1_sb, xnd, acc, tabs)
            experts(nc, cst, w_sb, b2_sb, w_in, w1, w2, b2, b1_sb, xnd, acc, tabs)
        finish(nc, xs, cst, res, acc, a["L0_ffn_Wp1"], a["L0_ffn_bp1"], a["L0_ffn_Wp2"], a["L0_ffn_bp2"], out)


def const_table():
    import numpy as np
    c = np.zeros((P, NCONST), np.float32)
    p = np.arange(P)
    c[:, C_ID:C_ID + P] = p[:, None] == p[None]
    c[:, C_UP:C_UP + P] = p[:, None] < p[None]
    c[:, C_ONE:C_ONE + P] = 1
    c[:, C_IOTA:C_IOTA + P] = p[None]
    theta = (np.float32(1.0) / np.float32(10000.0) ** (np.arange(0, HD, 2, dtype=np.float32) / np.float32(HD)))
    key_pos = np.where(p < START, p, S - NK + p)
    for j, pos in enumerate((p, P + p, key_pos)):
        angle = (pos.astype(np.float32)[:, None] * theta[None]).astype(np.float32)
        c[:, C_ROPE + j * HD:C_ROPE + j * HD + HD // 2] = np.cos(angle)
        c[:, C_ROPE + j * HD + HD // 2:C_ROPE + (j + 1) * HD] = np.sin(angle)
    e = np.arange(E)
    c[:, C_LOW:C_LOW + E * E] = (e[None, :] < e[:, None]).reshape(1, E * E)
    c[:, C_TOK:C_TOK + NT] = 1 + p[:, None] + P * np.arange(NT)[None]
    c[:, C_TRASH] = TRASH + p
    return c


def kernel(**inputs):
    import numpy as _np
    import concourse.bacc as _bacc
    from concourse import mybir as _mybir
    from concourse.bass_utils import run_bass_kernel_spmd as _run

    arrays = {n: _np.ascontiguousarray(a) for n, a in inputs.items()}
    for n in ("Wq", "Wk", "Wv", "Wo"):
        arrays[f"L0_attn_{n}"] = _np.ascontiguousarray(arrays[f"L0_attn_{n}"].T)
    c = arrays.pop("ctx_2048").reshape(B, SH, CH, LB, P)[..., ::-1].transpose(1, 4, 3, 0, 2)
    arrays["ctx_rev"] = _np.ascontiguousarray(_np.concatenate([c, c[..., :CE - CH]], axis=-1)).reshape(SH, P, -1)
    arrays["L0_ffn_b1"] = _np.ascontiguousarray(arrays["L0_ffn_b1"].reshape(E, KF, P).transpose(2, 0, 1)).reshape(P, -1)
    for n in ("bp1", "Wp2"):
        arrays[f"L0_ffn_{n}"] = _np.ascontiguousarray(arrays[f"L0_ffn_{n}"].reshape(-1, P).T)
    arrays["consts"] = const_table()

    nc = _bacc.Bacc("TRN2", target_bir_lowering=False, num_devices=1)
    feeds, args = {}, {}
    for n, a in arrays.items():
        feeds[f"in_{n}"] = a
        args[n] = nc.dram_tensor(f"in_{n}", a.shape, _mybir.dt.from_np(a.dtype), kind="ExternalInput").ap()
    out = nc.dram_tensor("out_0", (B, S, D), F32, kind="ExternalOutput").ap()
    decoder_layer(nc, out, **args)
    r = _run(nc, [feeds], core_ids=[0])
    return r.results[0]["out_0"]
```

```python
from contextlib import ExitStack

import concourse.bass as bass
from concourse import mybir

F32 = mybir.dt.float32
F32R = mybir.dt.float32r
I32 = mybir.dt.int32
U32 = mybir.dt.uint32
ACT = mybir.ActivationFunctionType
ALU = mybir.AluOpType
AX_X = mybir.AxisListType.X

P = 128
B, S, D = 8, 256, 512
KD = D // P
TPB = S // P
NT = B * TPB
HEADS = 16
HD = D // HEADS
START, RECENT = 26, 64
NK = START + RECENT
SCALE = float(HD) ** -0.5
EPS = 1e-5

SH = 32
CH = 8
LB = D // P
ND = 5
CE = CH + ND - 1
QE = 2 * CH
KPAD = 640

E, TOPK = 12, 3
FF = 1280
KF = FF // P
NTILE = NT * TOPK + E
TRASH = NT * P
WS = KD * FF + KF * D
WC = 512
NCHUNK = WS // WC

C_ID = 0
C_UP = C_ID + P
C_ONE = C_UP + P
C_IOTA = C_ONE + P
C_ROPE = C_IOTA + P
C_LOW = C_ROPE + 3 * HD
C_TOK = C_LOW + E * E
C_TRASH = C_TOK + NT
NCONST = C_TRASH + 1


def view(ap, off, dims):
    return bass.AP(tensor=ap.tensor, offset=ap.offset + off, ap=[ap.ap[0]] + [list(d) for d in dims])


def bc(ap, n):
    return bass.AP(tensor=ap.tensor, offset=ap.offset, ap=[list(d) for d in ap.ap] + [[0, n]])


class Steps:

    def __init__(self, eng, sem, base=0):
        self.eng, self.sem, self.base, self.n = eng, sem, base, 0

    def do(self, ins):
        self.n += 1
        ins.then_inc(self.sem, 1)
        self.eng.wait_ge(self.sem, self.base + self.n)


def attention(nc, xs, cst, x, wqT, wkT, wvT, woT, bq, bk, bv, bo, consts, stats1):
    with ExitStack() as ctx:
        def sb(name, shape, dt=F32):
            return ctx.enter_context(nc.sbuf_tensor(name, shape, dt))

        def psum(name, shape):
            return ctx.enter_context(nc.psum_tensor(name, shape, F32))

        def sem(name):
            return ctx.enter_context(nc.semaphore(name))

        wq, wk, wv, wo = (sb(n, [P, KD * D]) for n in ("wq", "wk", "wv", "wo"))
        bias_q, bias_k, bias_v, bias_o = (sb(n, [P, D]) for n in ("bias_q", "bias_k", "bias_v", "bias_o"))
        stats = sb("stats", [P, NT, 6])
        mv = sb("mv", [P, NT, 2])
        rstd = sb("rstd", [P, NT])
        xn = sb("xn", [P, TPB, D])
        xT = sb("xT", [P, TPB, KD, P])
        xkT = sb("xkT", [P, KD, NK])
        qkb = sb("qkb", [P, 3, D])
        rc = sb("rc", [P, D])
        rs = sb("rs", [P, D])
        qkr = sb("qkr", [P, 3, D])
        qT = sb("qT", [P, TPB, KD, P])
        kT = sb("kT", [P, KD, NK])
        vv = sb("vv", [NK, D])
        mx = sb("mx", [P, HEADS])
        sx = sb("sx", [P, TPB, HEADS * NK])
        pm = sb("pm", [P, TPB, HEADS * NK])
        den = sb("den", [P, TPB, HEADS])
        rden = sb("rden", [P, TPB, HEADS])
        pT = sb("pT", [NK, HEADS * P])
        oT = sb("oT", [P, KD, P])
        yo = sb("yo", [P, D])

        ps_t = psum("ps_t", [P, 512])
        ps_p = psum("ps_p", [P, 2, 512])
        ps_s = psum("ps_s", [P, 4, 512])
        ps_o = psum("ps_o", [P, KD, P])

        x_in = [sem(f"x_in{i}") for i in range(4)]
        c_in, wq_in, wk_in, wv_in, wo_in, b_in = (sem(n) for n in ("c_in", "wq_in", "wk_in", "wv_in", "wo_in", "b_in"))
        var_ready = sem("var_ready")
        std_ready = sem("std_ready")
        xn_ready = sem("xn_ready")
        xt_done = sem("xt_done")
        qkt_done = sem("qkt_done")
        t_evac = sem("t_evac")
        qkv_done = sem("qkv_done")
        wo_done = sem("wo_done")
        p_evac = sem("p_evac")
        roped = sem("roped")
        s_done = sem("s_done")
        sx_ready = sem("sx_ready")
        exp_done = sem("exp_done")
        pt_done = sem("pt_done")
        p_ready = sem("p_ready")
        pt_evac = sem("pt_evac")
        pv_done = sem("pv_done")
        o_evac = sem("o_evac")
        dve_step = sem("dve_step")
        pool_step = sem("pool_step")
        stats_done = sem("stats_done")
        aggr_done = sem("aggr_done")

        def t_xt(b, t):
            return 5 * b + t

        def t_qk(b, j):
            return 5 * b + 2 + j

        def p_qkv(b, j):
            return 4 + 6 * (b - 1) + (0, 1, 2, 4)[j] if not isinstance(b, int) or b else j

        def p_wo(b, t, last):
            return 4 + 6 * b + (t if last else (3, 5)[t])

        bank_qkv0, bank_qkv, bank_wo, bank_wo_last = (0, 1, 0, 1), (0, 1, 0, 0), (1, 1), (0, 1)

        def half(buf, t, f):
            return buf[:, t, f * 8 * NK:(f + 1) * 8 * NK]

        block = ctx.enter_context(nc.Block())

        @block.sync
        def _(sp):
            xt = x.rearrange("b (t p) d -> p (b t) d", p=P)
            for i in range(4):
                sp.dma_start(xs[:, 4 * i:4 * i + 4, :], xt[:, 4 * i:4 * i + 4, :]).then_inc(x_in[i], 16)
            for w, src, s in ((wq, wqT, wq_in), (wk, wkT, wk_in), (wv, wvT, wv_in), (wo, woT, wo_in)):
                sp.dma_start(w[:].rearrange("p (k n) -> p k n", k=KD),
                             src.rearrange("(k p) n -> p k n", p=P)).then_inc(s, 16)

        @block.scalar
        def _(act):
            act.dma_start(cst[:], consts).then_inc(c_in, 16)
            for t, src in ((bias_q, bq), (bias_k, bk), (bias_v, bv), (bias_o, bo)):
                act.dma_start(t[:], src.partition_broadcast(P)).then_inc(b_in, 16)
            act.wait_ge(var_ready, 1)
            nc.scalar.activation(rstd[:], rstd[:], ACT.Sqrt).then_inc(std_ready, 1)

            act.sem_inc(pt_evac, 1)
            act.sem_inc(o_evac, 1)

            def evac(done, n, dst, src):
                act.wait_ge(done, n)
                nc.scalar.activation(dst, src, ACT.Copy).then_inc(t_evac, 1)

            def evac_x(b, t):
                lo, hi, at = ((0, START, 0), (P - RECENT, P, START))[t]
                act.wait_ge(xt_done, 2 * b + t + 1)
                ps = ps_t[:].rearrange("p (k n) -> p k n", k=KD)
                nc.scalar.activation(xkT[:, :, at:at + hi - lo], ps[:, :, lo:hi], ACT.Copy)
                nc.scalar.activation(xT[:, t], ps, ACT.Copy).then_inc(t_evac, 1)

            def evac_qk(b):
                for t in range(TPB):
                    evac(qkt_done, 3 * b + t + 1, qT[:, t].rearrange("p k n -> p (k n)"), ps_t[:])
                evac(qkt_done, 3 * b + 3, kT[:], ps_t[:].rearrange("p (k n) -> p k n", k=KD)[:, :, 0:NK])

            def exps(b, t):
                for f in range(2):
                    act.wait_ge(sx_ready, 4 * b + 2 * t + f + 1)
                    nc.scalar.activation(half(pm, t, f), half(sx, t, f), ACT.Exp, scale=SCALE).then_inc(exp_done, 1)

            def evac_pt(b, t):
                for f in range(2):
                    act.wait_ge(pt_done, 4 * b + 2 * t + f + 1)
                    nc.scalar.activation(view(pT[:], f * 8 * P, [[4 * P, 2], [1, 4 * P]]),
                                         ps_s[0:NK, 2 * f:2 * f + 2], ACT.Copy).then_inc(pt_evac, 1)

            def evac_o(b, t):
                act.wait_ge(pv_done, 2 * b + t + 1)
                nc.scalar.activation(oT[:], ps_o[:], ACT.Copy).then_inc(o_evac, 1)

            def batch(b, last):
                if not last:
                    evac_x(b + 1, 0)
                    evac_x(b + 1, 1)
                exps(b, 0)
                evac_pt(b, 0)
                evac_o(b, 0)
                exps(b, 1)
                if not last:
                    evac_qk(b + 1)
                evac_pt(b, 1)
                evac_o(b, 1)

            evac_x(0, 0)
            evac_x(0, 1)
            evac_qk(0)
            with act.Fori(0, B - 1) as b:
                batch(b, False)
            batch(B - 1, True)

        @block.gpsimd
        def _(pool):
            def rope(b, j, steps):
                idx = p_qkv(b, j)
                pool.wait_ge(p_evac, idx + 1)
                if not isinstance(b, int) or b:
                    pool.wait_ge(qkt_done, 3 * b + j - 2)
                n = P if j < 2 else NK
                src = qkb[0:n, j]
                out = qkr[0:n, j]
                cos = view(cst[0:n], C_ROPE + j * HD, [[0, HEADS], [1, HD // 2], [0, 2]])
                sin = view(cst[0:n], C_ROPE + j * HD + HD // 2, [[0, HEADS], [1, HD // 2]])

                def pair(a, k):
                    return view(a, k, [[HD, HEADS], [2, HD // 2]])

                def full(a):
                    return view(a, 0, [[HD, HEADS], [2, HD // 2], [1, 2]])

                nc.gpsimd.tensor_tensor(pair(rs[0:n], 0), pair(src, 1), sin, ALU.mult)
                nc.gpsimd.tensor_tensor(pair(rs[0:n], 1), pair(src, 0), sin, ALU.mult)
                steps.do(nc.gpsimd.tensor_tensor(full(rc[0:n]), full(src), cos, ALU.mult))
                nc.gpsimd.tensor_tensor(pair(out, 0), pair(rc[0:n], 0), pair(rs[0:n], 0), ALU.subtract)
                nc.gpsimd.tensor_tensor(pair(out, 1), pair(rc[0:n], 1), pair(rs[0:n], 1), ALU.add)\
                    .then_inc(roped, 1)
                pool.wait_ge(roped, roped_index(b, j) + 1)

            def roped_index(b, j):
                return 3 * b + j

            pool.wait_ge(c_in, 16)
            first = Steps(pool, pool_step)
            for j in range(3):
                rope(0, j, first)
            with pool.Fori(0, B - 1) as b:
                loop = Steps(pool, pool_step, base=first.n + 3 * b)
                for j in range(3):
                    rope(b + 1, j, loop)

        @block.vector
        def _(dve):
            for i in range(4):
                dve.wait_ge(x_in[i], 16)
                with dve.Fori(4 * i, 4 * i + 4) as t:
                    nc.vector.bn_stats(stats[:, t], xs[:, t]).then_inc(stats_done, 1)
            dve.wait_ge(stats_done, NT)
            for t in range(NT):
                nc.vector.bn_aggr(mv[:, t], stats[:, t]).then_inc(aggr_done, 1)
            dve.wait_ge(aggr_done, NT)
            steps = Steps(dve, dve_step)
            nc.vector.tensor_scalar(rstd[:], mv[:, :, 1], EPS, None, ALU.add).then_inc(var_ready, 1)
            dve.wait_ge(std_ready, 1)
            steps.do(nc.vector.reciprocal(rstd[:], rstd[:]))
            dve.wait_ge(b_in, 64)

            def normalise(b, t):
                if not isinstance(b, int) or b:
                    dve.wait_ge(xt_done, 2 * b + t - 1)
                i = 2 * b + t
                nc.vector.tensor_scalar(xn[:, t], xs[:, i], mv[:, i, 0:1], rstd[:, bass.ds(i, 1)],
                                        ALU.subtract, ALU.mult).then_inc(xn_ready, 1)

            def add_bias(b, j, bank):
                dve.wait_ge(qkv_done, 4 * b + j + 1)
                n = P if j < 2 else NK
                if j < 3 and (not isinstance(b, int) or b):
                    dve.wait_ge(roped, 3 * b + j - 2)
                dst = vv[:] if j == 3 else qkb[0:n, j]
                bias = (bias_q, bias_q, bias_k, bias_v)[j]
                nc.vector.tensor_tensor(dst, ps_p[0:n, bank], bias[0:n], ALU.add).then_inc(p_evac, 1)

            def softmax_top(b, t, steps):
                dve.wait_ge(s_done, 2 * b + t + 1)
                for f in range(2):
                    sc = view(ps_s[:], f * 1024, [[512, 2], [NK, 4], [1, NK]])
                    steps.do(nc.vector.tensor_reduce(view(mx[:], 8 * f, [[4, 2], [1, 4]]), sc, AX_X, ALU.max))
                    nc.vector.tensor_tensor(view(half(sx, t, f), 0, [[4 * NK, 2], [NK, 4], [1, NK]]), sc,
                                            view(mx[:], 8 * f, [[4, 2], [1, 4], [0, NK]]), ALU.subtract)\
                        .then_inc(sx_ready, 1)
                dve.wait_ge(sx_ready, 4 * b + 2 * t + 2)

            def softmax_sum(b, t, steps):
                for f in range(2):
                    dve.wait_ge(exp_done, 4 * b + 2 * t + f + 1)
                    probs = view(half(pm, t, f), 0, [[NK, 8], [1, NK]])
                    d, rd = den[:, t, 8 * f:8 * f + 8], rden[:, t, 8 * f:8 * f + 8]
                    steps.do(nc.vector.tensor_reduce(d, probs, AX_X, ALU.add))
                    steps.do(nc.vector.reciprocal(rd, d))
                    nc.vector.tensor_tensor(probs, probs, bc(rd, NK), ALU.mult).then_inc(p_ready, 1)

            def residual(b, t, last, steps):
                dve.wait_ge(wo_done, 2 * b + t + 1)
                i = 2 * b + t
                bank = (bank_wo_last if last else bank_wo)[t]
                ins = nc.vector.tensor_tensor(yo[:], ps_p[:, bank], bias_o[:], ALU.add)
                ins.then_inc(p_evac, 1)
                dve.wait_ge(p_evac, p_wo(b, t, last) + 1)
                steps.do(nc.vector.tensor_tensor(xs[:, i], xs[:, i], yo[:], ALU.add))
                nc.vector.bn_stats(stats1[:, i], xs[:, i])

            def batch(b, last, steps):
                if not last:
                    normalise(b + 1, 0)
                    normalise(b + 1, 1)
                softmax_top(b, 0, steps)
                if not last:
                    add_bias(b + 1, 0, bank_qkv[0])
                softmax_sum(b, 0, steps)
                if not last:
                    add_bias(b + 1, 1, bank_qkv[1])
                    add_bias(b + 1, 2, bank_qkv[2])
                softmax_top(b, 1, steps)
                residual(b, 0, last, steps)
                softmax_sum(b, 1, steps)
                if not last:
                    add_bias(b + 1, 3, bank_qkv[3])
                residual(b, 1, last, steps)

            normalise(0, 0)
            normalise(0, 1)
            for j in range(4):
                add_bias(0, j, bank_qkv0[j])
            per_batch = 14
            with dve.Fori(0, B - 1) as b:
                loop = Steps(dve, dve_step, base=steps.n + per_batch * b)
                batch(b, False, loop)
            assert loop.n == per_batch, loop.n
            tail = Steps(dve, dve_step, base=steps.n + per_batch * (B - 1))
            batch(B - 1, True, tail)

        @block.tensor
        def _(pe):
            pe.wait_ge(c_in, 16)
            ident = cst[:, C_ID:C_ID + P]

            def free_t(idx):
                if not isinstance(idx, int) or idx:
                    pe.wait_ge(t_evac, idx)

            def free_p(idx):
                if not isinstance(idx, int) or idx > 1:
                    pe.wait_ge(p_evac, idx - 1)

            def transposes(idx, done, src, rows):
                free_t(idx)
                for k in range(KD):
                    last = nc.tensor.transpose(ps_t[:, k * P:k * P + rows], src[0:rows, k * P:(k + 1) * P],
                                               ident[0:rows, 0:rows])
                last.then_inc(done, 1)

            def x_t(b, t):
                pe.wait_ge(xn_ready, 2 * b + t + 1)
                transposes(t_xt(b, t), xt_done, xn[:, t], P)

            def qk_t(b):
                for j in range(3):
                    pe.wait_ge(roped, 3 * b + j + 1)
                    transposes(t_qk(b, j), qkt_done, qkr[:, j], P if j < 2 else NK)

            def project(b, j, bank):
                free_p(p_qkv(b, j))
                pe.wait_ge(t_evac, t_xt(b, 1 if j else 0) + 1)
                w = (wq, wq, wk, wv)[j]
                n = P if j < 2 else NK
                for k in range(KD):
                    lhs = xT[:, j, k] if j < 2 else xkT[:, k]
                    last = nc.tensor.matmul(ps_p[0:n, bank], lhs, w[:, k * D:(k + 1) * D],
                                            start=(k == 0), stop=(k == KD - 1))
                last.then_inc(qkv_done, 1)

            def w_o(b, t, last):
                idx = p_wo(b, t, last)
                free_p(idx)
                pe.wait_ge(o_evac, 2 * b + t + 2)
                for k in range(KD):
                    mm = nc.tensor.matmul(ps_p[:, (bank_wo_last if last else bank_wo)[t]], oT[:, k],
                                          wo[:, k * D:(k + 1) * D], start=(k == 0), stop=(k == KD - 1))
                mm.then_inc(wo_done, 1)

            def scores(b, t):
                if t == 0:
                    pe.wait_ge(t_evac, t_qk(b, 2) + 1)
                pe.wait_ge(pt_evac, 4 * b + 2 * t + 1)
                for k in range(KD):
                    for g in range(4):
                        last = nc.tensor.matmul(ps_s[:, g, k * NK:(k + 1) * NK],
                                                qT[g * HD:(g + 1) * HD, t, k], kT[g * HD:(g + 1) * HD, k],
                                                start=True, stop=True)
                last.then_inc(s_done, 1)

            def p_t(b, t):
                for f in range(2):
                    pe.wait_ge(p_ready, 4 * b + 2 * t + f + 1)
                    for h in range(8 * f, 8 * f + 8):
                        last = nc.tensor.transpose(ps_s[0:NK, h // 4, (h % 4) * P:(h % 4 + 1) * P],
                                                   pm[:, t, h * NK:(h + 1) * NK], ident)
                    last.then_inc(pt_done, 1)

            def p_v(b, t):
                pe.wait_ge(pt_evac, 4 * b + 2 * t + 3)
                if t == 0:
                    pe.wait_ge(p_evac, 4 + 6 * b)
                pe.wait_ge(o_evac, 2 * b + t + 1)
                for k in range(KD):
                    for g in range(4):
                        head, at = 4 * k + g, (4 * g + k) * P
                        last = nc.tensor.matmul(ps_o[g * HD:(g + 1) * HD, k], vv[:, head * HD:(head + 1) * HD],
                                                pT[:, at:at + P], start=True, stop=True)
                last.then_inc(pv_done, 1)

            def batch(b, last):
                scores(b, 0)
                if not last:
                    x_t(b + 1, 0)
                    x_t(b + 1, 1)
                    project(b + 1, 0, bank_qkv[0])
                    project(b + 1, 1, bank_qkv[1])
                p_t(b, 0)
                if not last:
                    project(b + 1, 2, bank_qkv[2])
                scores(b, 1)
                p_v(b, 0)
                w_o(b, 0, last)
                if not last:
                    qk_t(b + 1)
                p_t(b, 1)
                p_v(b, 1)
                if not last:
                    project(b + 1, 3, bank_qkv[3])
                w_o(b, 1, last)

            x_t(0, 0)
            x_t(0, 1)
            pe.wait_ge(wq_in, 16)
            project(0, 0, bank_qkv0[0])
            project(0, 1, bank_qkv0[1])
            pe.wait_ge(wk_in, 16)
            project(0, 2, bank_qkv0[2])
            pe.wait_ge(wv_in, 16)
            project(0, 3, bank_qkv0[3])
            qk_t(0)
            pe.wait_ge(wo_in, 16)
            with pe.Fori(0, B - 1) as b:
                batch(b, False)
            batch(B - 1, True)


def convolution(nc, xs, cst, stats1, res, ctx_rev, taps, diag, kpad):
    with ExitStack() as ctx:
        def sb(name, shape, dt=F32):
            return ctx.enter_context(nc.sbuf_tensor(name, shape, dt))

        def psum(name, shape):
            return ctx.enter_context(nc.psum_tensor(name, shape, F32))

        def sem(name):
            return ctx.enter_context(nc.semaphore(name))

        NCOL = B * ND * CH
        mv = sb("mv_b", [P, NT, 2])
        rstd = sb("rstd_b", [P, NT])
        xn = sb("xn_b", [P, 2, D])
        qe = sb("qe", [P, LB * B * SH * QE])
        kp = sb("kp", [SH, KPAD])
        dd = sb("dd", [SH, 1])
        toe = sb("toe", [P, 2, D])
        cc = sb("cc", [P, 2, LB * B * CE])
        kv = sb("kv", [P, 2, LB * NCOL])
        ye = sb("ye", [P, 2, LB * B * ND * QE])
        prod = sb("prod", [P, LB * B * CH * CH])
        ps = psum("ps_b", [P, 8, 512])

        taps_in, pad_zero, pad_ready, pad_out = (sem(n) for n in ("taps_in", "pad_zero", "pad_ready", "pad_out"))
        aggr = sem("aggr_b")
        var_ready, std_ready = sem("var_ready_b"), sem("std_ready_b")
        dve_step = sem("dve_step_b")
        xn_ready = sem("xn_ready_b")
        xt_done = sem("xt_done_b")
        even_copied = sem("even_copied")
        odd_copied = sem("odd_copied")
        head_in = [sem("head_in0"), sem("head_in1")]
        kv_ready = sem("kv_ready")
        conv_done = sem("conv_done")
        ye_ready = sem("ye_ready")
        prod_ready = sem("prod_ready")
        res_ready = sem("res_ready")

        block = ctx.enter_context(nc.Block())

        @block.sync
        def _(sp):
            sp.dma_start(dd[:], diag.rearrange("(h a) -> h a", a=1)).then_inc(taps_in, 16)
            sp.wait_ge(pad_zero, 1)
            sp.dma_start(kp[:, P - 1:P - 1 + D], taps).then_inc(taps_in, 16)
            sp.wait_ge(pad_ready, 1)
            sp.dma_start(kpad, kp[:]).then_inc(pad_out, 16)
            sp.wait_ge(pad_out, 16)

            def load(h, par, first):
                at, row = h * KPAD, h * (P * LB * B * CE)
                if not first:
                    at, row, n = sp.snap(at), sp.snap(row), sp.snap(h + 1)
                    sp.wait_ge(kv_ready, n)
                    sp.wait_ge(conv_done, n)
                sp.dma_start(toe[:, par], bass.AP(tensor=kpad.tensor, offset=at, ap=[[1, P], [1, D]]))\
                    .then_inc(head_in[par], 16)
                sp.dma_start(cc[:, par], bass.AP(tensor=ctx_rev.tensor, offset=row,
                                                 ap=[[LB * B * CE, P], [1, LB * B * CE]])).then_inc(head_in[par], 16)

            load(0, 0, True)
            load(1, 1, True)
            with sp.Fori(1, SH // 2) as i:
                load(2 * i, 0, False)
                load(2 * i + 1, 1, False)

        @block.gpsimd
        def _(pool):
            pool.sem_inc(kv_ready, 2)
            nc.gpsimd.memset(kp[:], 0.0).then_inc(pad_zero, 1)

            def multiply(i, par):
                h = 2 * i + par
                pool.wait_ge(head_in[par], 32 * i + 32)
                pool.wait_ge(conv_done, h + 1)
                c = cc[:, par]
                nc.gpsimd.tensor_tensor(
                    view(kv[:, par], 0, [[ND * CH, LB * B], [CH, ND], [1, CH]]),
                    view(c, 0, [[CE, LB * B], [0, ND], [1, CH]]),
                    view(c, 0, [[CE, LB * B], [1, ND], [1, CH]]), ALU.mult).then_inc(kv_ready, 1)

            with pool.Fori(0, SH // 2) as i:
                multiply(i, 0)
                multiply(i, 1)

        @block.scalar
        def _(act):
            act.sem_inc(even_copied, 1)
            act.sem_inc(ye_ready, 2)
            act.wait_ge(var_ready, 1)
            nc.scalar.activation(rstd[:], rstd[:], ACT.Sqrt).then_inc(std_ready, 1)
            with act.Fori(0, B) as b:
                act.wait_ge(xt_done, 2 * b + 1)
                nc.scalar.activation(q_tile(qe, b, 0, 0), ps_tile(ps, 0), ACT.Copy)
                nc.scalar.activation(q_tile(qe, b, 0, CH), ps_tile(ps, 0), ACT.Copy).then_inc(even_copied, 1)

            def evacuate(h, par):
                act.wait_ge(conv_done, h + 3)
                act.wait_ge(prod_ready, h + 1)
                y = view(ps[:], 4 * par * 512, [[512, LB], [CH, B * ND], [1, CH]])
                for copy in range(2):
                    ins = nc.scalar.activation(
                        view(ye[:, par], copy * CH, [[B * ND * QE, LB], [QE, B * ND], [1, CH]]), y, ACT.Copy)
                ins.then_inc(ye_ready, 1)

            with act.Fori(0, SH // 2) as i:
                evacuate(2 * i, 0)
                evacuate(2 * i + 1, 1)

        @block.tensor
        def _(pe):
            ident = cst[:, C_ID:C_ID + P]
            pe.sem_inc(conv_done, 2)
            with pe.Fori(0, B) as b:
                for t in range(TPB):
                    pe.wait_ge(xn_ready, 2 * b + t + 1)
                    pe.wait_ge((even_copied, odd_copied)[t], b + 1)
                    for k in range(KD):
                        last = nc.tensor.transpose(ps[:, t, k * P:(k + 1) * P], xn[:, t, k * P:(k + 1) * P], ident)
                    last.then_inc(xt_done, 1)

            def convolve(h, i, par):
                pe.wait_ge(head_in[par], 32 * i + 32)
                pe.wait_ge(kv_ready, h + 3)
                pe.wait_ge(ye_ready, h + 1)
                for l in range(LB):
                    for m in range(l + 1):
                        last = nc.tensor.matmul(ps[:, 4 * par + l, 0:NCOL], toe[:, par, (l - m) * P:(l - m + 1) * P],
                                                kv[:, par, m * NCOL:(m + 1) * NCOL],
                                                start=(m == 0), stop=(m == l))
                last.then_inc(conv_done, 1)

            pe.wait_ge(even_copied, B + 1)
            pe.wait_ge(odd_copied, B + 1)
            with pe.Fori(0, SH // 2) as i:
                convolve(2 * i, i, 0)
                convolve(2 * i + 1, i, 1)

        @block.vector
        def _(dve):
            dve.sem_inc(odd_copied, 1)
            dve.sem_inc(prod_ready, 2)
            dve.wait_ge(taps_in, 32)
            nc.vector.tensor_tensor(kp[:, P - 1:P], kp[:, P - 1:P], dd[:], ALU.add).then_inc(pad_ready, 1)
            steps = Steps(dve, dve_step)
            for t in range(NT):
                nc.vector.bn_aggr(mv[:, t], stats1[:, t]).then_inc(aggr, 1)
            dve.wait_ge(aggr, NT)
            nc.vector.tensor_scalar(rstd[:], mv[:, :, 1], EPS, None, ALU.add).then_inc(var_ready, 1)
            dve.wait_ge(std_ready, 1)
            steps.do(nc.vector.reciprocal(rstd[:], rstd[:]))

            def normalise(b, t, first):
                if not first:
                    dve.wait_ge(xt_done, 2 * b + t - 1)
                i = 2 * b + t
                nc.vector.tensor_scalar(xn[:, t], xs[:, i], mv[:, i, 0:1], rstd[:, bass.ds(i, 1)],
                                        ALU.subtract, ALU.mult).then_inc(xn_ready, 1)

            def copy_odd(b):
                dve.wait_ge(xt_done, 2 * b + 2)
                nc.vector.tensor_copy(q_tile(qe, b, 1, 0), ps_tile(ps, 1))
                nc.vector.tensor_copy(q_tile(qe, b, 1, CH), ps_tile(ps, 1)).then_inc(odd_copied, 1)

            normalise(0, 0, True)
            normalise(0, 1, True)
            with dve.Fori(0, B - 1) as b:
                normalise(b + 1, 0, False)
                copy_odd(b)
                normalise(b + 1, 1, False)
            copy_odd(B - 1)
            dve.wait_ge(even_copied, B + 1)
            dve.wait_ge(odd_copied, B + 1)

            def contract(h, par):
                dve.wait_ge(ye_ready, h + 3)
                q = qe[:]
                y = ye[:, par]
                o = prod[:]
                lb_q, lb_y, lb_o = [SH * QE, LB * B], [ND * QE, LB * B], [CH * CH, LB * B]
                nc.vector.tensor_tensor(view(o, 0, [lb_o, [CH, ND], [1, CH]]),
                                        view(y, 0, [lb_y, [QE, ND], [1, CH]]),
                                        view(q, h * QE, [lb_q, [1, ND], [1, CH]]), ALU.mult)
                nc.vector.tensor_tensor(view(o, ND * CH, [lb_o, [CH, CH - ND], [1, CH]]),
                                        view(y, 3 * (QE - 1) + CH, [lb_y, [1 - QE, CH - ND], [1, CH]]),
                                        view(q, h * QE + CH - 3, [lb_q, [1, CH - ND], [1, CH]]), ALU.mult)\
                    .then_inc(prod_ready, 1)
                dve.wait_ge(prod_ready, h + 3)
                nc.vector.tensor_reduce(view(res[:], h * CH, [[S, LB * B], [1, CH]]),
                                        view(o, 0, [lb_o, [1, CH], [CH, CH]]), AX_X, ALU.add).then_inc(res_ready, 1)
                dve.wait_ge(res_ready, h + 1)

            with dve.Fori(0, SH // 2) as i:
                contract(2 * i, 0)
                contract(2 * i + 1, 1)


def q_tile(qe, b, t, at):
    return view(qe[:], b * (SH * QE) + t * (SH // 2) * QE + at, [[B * SH * QE, LB], [QE, SH // 2], [1, CH]])


def ps_tile(ps, t):
    return view(ps[:], t * 512, [[P, LB], [CH, SH // 2], [1, CH]])


def logits_phase(nc, xs, cst, res, prob, wr, br, b1, b1_sb, x2d, xnd, acc):
    with ExitStack() as ctx:
        def sb(name, shape, dt=F32):
            return ctx.enter_context(nc.sbuf_tensor(name, shape, dt))

        def psum(name, shape):
            return ctx.enter_context(nc.psum_tensor(name, shape, F32))

        def sem(name):
            return ctx.enter_context(nc.semaphore(name))

        stats = sb("stats_c", [P, NT, 6])
        mv = sb("mv_c", [P, NT, 2])
        rstd = sb("rstd_c", [P, NT])
        wr_sb = sb("wr_sb", [P, KD * E])
        br_sb = sb("br_sb", [P, E])
        xn = sb("xn_c", [P, TPB, D])
        xT = sb("xT_c", [P, TPB, KD * P])
        zeros = sb("zeros", [P, D])

        ps_r = psum("ps_r", [P, 2, 512])
        ps_x = psum("ps_x", [P, 2, 512])
        ps_l = psum("ps_l", [P, 2, 512])

        small_in, zeroed, acc_out = sem("small_in"), sem("zeroed"), sem("acc_out")
        rt_done = sem("rt_done")
        x2_ready = sem("x2_ready")
        aggr = sem("aggr_c")
        var_ready, std_ready = sem("var_ready_c"), sem("std_ready_c")
        dve_step = sem("dve_step_c")
        xn_ready = sem("xn_ready_c")
        xt_done = sem("xt_done_c")
        xt_evac = sem("xt_evac_c")
        logit_done = sem("logit_done")
        logit_read = sem("logit_read")
        xn_out = [sem("xn_out0"), sem("xn_out1")]
        x2_out = sem("x2_out")

        block = ctx.enter_context(nc.Block())

        @block.sync
        def _(sp):
            sp.dma_start(wr_sb[:].rearrange("p (k e) -> p k e", k=KD), wr.rearrange("(k p) e -> p k e", p=P))\
                .then_inc(small_in, 16)
            sp.dma_start(br_sb[:], br.partition_broadcast(P)).then_inc(small_in, 16)
            sp.dma_start(b1_sb[:], b1).then_inc(small_in, 16)
            def store(b, t, dram, src, ready, out):
                at = sp.snap((2 * b + t) * (P * D))
                n = sp.snap(2 * b + t + 1)
                sp.wait_ge(ready, n)
                sp.dma_start(bass.AP(tensor=dram.tensor, offset=at, ap=[[D, P], [1, D]]), src)\
                    .then_inc(out, 16)

            x2t = x2d.rearrange("(t p) d -> p t d", p=P)
            for i in range(4):
                sp.wait_ge(x2_ready, 4 * i + 4)
                sp.dma_start(x2t[:, 4 * i:4 * i + 4], xs[:, 4 * i:4 * i + 4]).then_inc(x2_out, 16)
            with sp.Fori(0, B) as b:
                for t in range(TPB):
                    store(b, t, xnd, xn[:, t], xn_ready, xn_out[t])
            sp.wait_ge(x2_out, 16 * 4)
            sp.wait_ge(xn_out[0], 16 * B)
            sp.wait_ge(xn_out[1], 16 * B)
            sp.wait_ge(small_in, 48)

        @block.gpsimd
        def _(pool):
            nc.gpsimd.memset(zeros[:], 0.0).then_inc(zeroed, 1)
            pool.wait_ge(zeroed, 1)
            pool.dma_start(acc.rearrange("(t p) d -> p t d", p=P), view(zeros[:], 0, [[0, NT + 1], [1, D]]))\
                .then_inc(acc_out, 16)
            pool.wait_ge(acc_out, 16)

        @block.scalar
        def _(act):
            act.sem_inc(xt_evac, 2)
            act.wait_ge(var_ready, 1)
            nc.scalar.activation(rstd[:], rstd[:], ACT.Sqrt).then_inc(std_ready, 1)

            def evacuate(b, t):
                act.wait_ge(xt_done, 2 * b + t + 1)
                act.wait_ge(logit_done, 2 * b + t + 1)
                nc.scalar.activation(xT[:, t], ps_x[:, t], ACT.Copy).then_inc(xt_evac, 1)

            with act.Fori(0, B) as b:
                evacuate(b, 0)
                evacuate(b, 1)

        @block.tensor
        def _(pe):
            ident = cst[:, C_ID:C_ID + P]
            pe.sem_inc(logit_done, 2)
            for i in range(NT):
                if i > 1:
                    pe.wait_ge(x2_ready, i - 1)
                for l in range(LB):
                    at = (l * B + i // TPB) * S + i % TPB * P
                    last = nc.tensor.transpose(ps_r[:, i % 2, l * P:(l + 1) * P], res[:, at:at + P], ident)
                last.then_inc(rt_done, 1)
            pe.wait_ge(small_in, 48)

            def transposes(b, t):
                pe.wait_ge(xn_ready, 2 * b + t + 1)
                pe.wait_ge(xt_evac, 2 * b + t + 1)
                for k in range(KD):
                    last = nc.tensor.transpose(ps_x[:, t, k * P:(k + 1) * P], xn[:, t, k * P:(k + 1) * P], ident)
                last.then_inc(xt_done, 1)

            def logits(b, t):
                pe.wait_ge(xt_evac, 2 * b + t + 3)
                pe.wait_ge(logit_read, 2 * b + t + 1)
                for k in range(KD):
                    last = nc.tensor.matmul(ps_l[:, t, 0:E], xT[:, t, k * P:(k + 1) * P],
                                            wr_sb[:, k * E:(k + 1) * E], start=(k == 0), stop=(k == KD - 1))
                last.then_inc(logit_done, 1)

            with pe.Fori(0, B) as b:
                transposes(b, 0)
                transposes(b, 1)
                logits(b, 0)
                logits(b, 1)

        @block.vector
        def _(dve):
            dve.sem_inc(logit_read, 2)
            v = nc.vector
            steps = Steps(dve, dve_step)
            do = steps.do

            def add_conv(b, t):
                i = 2 * b + t
                dve.wait_ge(rt_done, i + 1)
                v.tensor_tensor(xs[:, i], xs[:, i], ps_r[:, t], ALU.add).then_inc(x2_ready, 1)
                dve.wait_ge(x2_ready, i + 1)
                v.bn_stats(stats[:, i], xs[:, i]).then_inc(aggr, 1)

            with dve.Fori(0, B) as b:
                add_conv(b, 0)
                add_conv(b, 1)
            dve.wait_ge(aggr, NT)
            for t in range(NT):
                v.bn_aggr(mv[:, t], stats[:, t]).then_inc(aggr, 1)
            dve.wait_ge(aggr, 2 * NT)
            v.tensor_scalar(rstd[:], mv[:, :, 1], EPS, None, ALU.add).then_inc(var_ready, 1)
            dve.wait_ge(std_ready, 1)
            do(v.reciprocal(rstd[:], rstd[:]))

            def normalise(b, t, first):
                if not first:
                    dve.wait_ge(xt_done, 2 * b + t - 1)
                    dve.wait_ge(xn_out[t], 16 * b)
                i = 2 * b + t
                v.tensor_scalar(xn[:, t], xs[:, i], mv[:, i, 0:1], rstd[:, bass.ds(i, 1)],
                                ALU.subtract, ALU.mult).then_inc(xn_ready, 1)

            def take_logits(b, t):
                dve.wait_ge(logit_done, 2 * b + t + 3)
                v.tensor_tensor(prob[:, 2 * b + t], ps_l[:, t, 0:E], br_sb[:], ALU.add).then_inc(logit_read, 1)

            normalise(0, 0, True)
            normalise(0, 1, True)
            dve.wait_ge(small_in, 48)
            with dve.Fori(0, B - 1) as b:
                normalise(b + 1, 0, False)
                normalise(b + 1, 1, False)
                take_logits(b, 0)
                take_logits(b, 1)
            take_logits(B - 1, 0)
            take_logits(B - 1, 1)
            dve.wait_ge(logit_read, NT + 2)


def route(nc, cst, prob, w_hi, w_lo, stage, stage_in, split_done, wcat, b2, b2_sb, b2_in, tabs):
    gidx, sidx, wt, eid, tstart_i = tabs
    with ExitStack() as ctx:
        def sb(name, shape, dt=F32):
            return ctx.enter_context(nc.sbuf_tensor(name, shape, dt))

        def psum(name, shape):
            return ctx.enter_context(nc.psum_tensor(name, shape, F32))

        def sem(name):
            return ctx.enter_context(nc.semaphore(name))

        TE = NT * E
        ex = sb("ex", [P, NT, E])
        rank = sb("rank", [P, NT, E])
        sel = sb("sel", [P, NT, E])
        ew = sb("ew", [P, NT, E])
        slot = sb("slot", [P, NT, E])
        before = sb("before", [P, NT, E])
        col = sb("col", [P, 2, NT])
        cnt = sb("cnt", [P, 6, E])
        slot3 = sb("slot3", [P, TOPK, NT])
        slot3_i = sb("slot3_i", [P, 3, TOPK * NT], I32)
        slot3_f = sb("slot3_f", [P, 2, TOPK * NT])
        tile_f = sb("tile_f", [P, 3, NTILE])
        ONE_HOT = NT * (P + NTILE)
        work = sb("work", [P, 2 * ONE_HOT])
        ps_c = psum("ps_c", [P, 512])
        ps_m = psum("ps_m", [P, 512])
        ps_r = psum("ps_r2", [P, 1, 512])
        dve_step = sem("dve_step_r")
        exp_in, exp_out = sem("exp_in"), sem("exp_out")
        sel_ready, counted = sem("sel_ready"), sem("counted")
        hot_ready, hot_used = sem("hot_ready"), sem("hot_used")
        cast = sem("cast")

        block = ctx.enter_context(nc.Block())

        @block.sync
        def _(sp):
            sp.dma_start(b2_sb[:, 0], bass.AP(tensor=b2.tensor, offset=0, ap=[[0, P], [1, D]])).then_inc(b2_in, 16)
            for c in range(2):
                sp.dma_start(stage[:, c], wcat[0, :, c * WC:(c + 1) * WC]).then_inc(stage_in[c], 16)
            with sp.Fori(1, NCHUNK // 2) as c:
                for par in range(2):
                    at = sp.snap((2 * c + par) * WC)
                    n = sp.snap(2 * c + par - 1)
                    sp.wait_ge(split_done, n)
                    sp.dma_start(stage[:, par], bass.AP(tensor=wcat.tensor, offset=at, ap=[[WS, P], [1, WC]]))\
                        .then_inc(stage_in[par], 16)
            sp.wait_ge(b2_in, 16)
            sp.wait_ge(stage_in[0], 8 * NCHUNK)
            sp.wait_ge(stage_in[1], 8 * NCHUNK)

        @block.gpsimd
        def _(pool):
            with pool.Fori(0, NCHUNK // 2) as c:
                for par in range(2):
                    n = 2 * c + par
                    pool.wait_ge(cast, n + 1)
                    nc.gpsimd.tensor_tensor(w_lo[:, 0, bass.ds(n * WC, WC)], stage[:, par],
                                            w_hi[:, 0, bass.ds(n * WC, WC)].bitcast(F32), ALU.subtract)\
                        .then_inc(split_done, 1)

        @block.scalar
        def _(act):
            for n in range(2):
                act.wait_ge(exp_in, n + 1)
                nc.scalar.activation(ex[:], ex[:], ACT.Exp).then_inc(exp_out, 1)
            with act.Fori(0, NCHUNK // 2) as c:
                for par in range(2):
                    act.wait_ge(stage_in[par], 16 * c + 16)
                    nc.scalar.activation(w_hi[:, 0, bass.ds((2 * c + par) * WC, WC)], stage[:, par], ACT.Copy)\
                        .then_inc(cast, 1)

        @block.tensor
        def _(pe):
            pe.wait_ge(sel_ready, 1)
            flat = sel[:].rearrange("p t e -> p (t e)")
            nc.tensor.matmul(ps_c[:, 0:TE], cst[:, C_UP:C_UP + P], flat, start=True, stop=True)
            nc.tensor.matmul(ps_m[:, 0:TE], cst[:, C_ONE:C_ONE + P], flat, start=True, stop=True)
            nc.tensor.matmul(ps_m[:, TE:2 * TE], cst[:, C_ONE:C_ONE + P], ew[:].rearrange("p t e -> p (t e)"),
                             start=True, stop=True).then_inc(counted, 1)
            for k in range(TOPK):
                pe.wait_ge(hot_ready, k + 1)
                oc, oa = one_hots(work, k, ONE_HOT)
                for t in range(NT):
                    last = nc.tensor.matmul(ps_r[:, 0, 0:NTILE], oc[:, t * P:(t + 1) * P],
                                            oa[:, t * NTILE:(t + 1) * NTILE], start=(k == 0 and t == 0),
                                            stop=(k == TOPK - 1 and t == NT - 1))
                last.then_inc(hot_used, 1)

        @block.vector
        def _(dve):
            v = nc.vector
            steps = Steps(dve, dve_step)
            do = steps.do
            mx, den = col[:, 0], col[:, 1]
            do(v.tensor_reduce(mx, prob[:], AX_X, ALU.max))
            v.tensor_tensor(ex[:], prob[:], bc(mx, E), ALU.subtract).then_inc(exp_in, 1)
            dve.wait_ge(exp_out, 1)
            do(v.tensor_reduce(den, ex[:], AX_X, ALU.add))
            do(v.reciprocal(den, den))
            do(v.tensor_tensor(prob[:], ex[:], bc(den, E), ALU.mult))
            gt = view(work[:], 0, [[E * E, NT], [E, E], [1, E]])
            eq = view(work[:], NT * E * E, [[E * E, NT], [E, E], [1, E]])
            other = view(prob[:], 0, [[E, NT], [0, E], [1, E]])
            own = view(prob[:], 0, [[E, NT], [1, E], [0, E]])
            low = view(cst[:], C_LOW, [[0, NT], [E, E], [1, E]])
            v.tensor_tensor(gt, other, own, ALU.is_gt)
            do(v.tensor_tensor(eq, other, own, ALU.is_equal))
            do(v.tensor_tensor(eq, eq, low, ALU.mult))
            do(v.tensor_tensor(gt, gt, eq, ALU.add))
            do(v.tensor_reduce(rank[:], gt, AX_X, ALU.add))
            do(v.tensor_scalar(sel[:], rank[:], float(TOPK), None, ALU.is_lt))
            do(v.tensor_reduce(mx, prob[:], AX_X, ALU.max))
            v.tensor_tensor(ex[:], prob[:], bc(mx, E), ALU.subtract).then_inc(exp_in, 1)
            dve.wait_ge(exp_out, 2)
            do(v.tensor_tensor(ex[:], ex[:], sel[:], ALU.mult))
            do(v.tensor_reduce(den, ex[:], AX_X, ALU.add))
            do(v.reciprocal(den, den))
            v.tensor_tensor(ew[:], ex[:], bc(den, E), ALU.mult).then_inc(sel_ready, 1)
            dve.wait_ge(counted, 1)

            count, inv, weight, ntile, tstart, tend = (cnt[:, i] for i in range(6))
            do(v.memset(before[:, 0], 0.0))
            for t in range(1, NT):
                do(v.tensor_tensor(before[:, t], before[:, t - 1], ps_m[:, (t - 1) * E:t * E], ALU.add))
            do(v.tensor_tensor(count, before[:, NT - 1], ps_m[:, (NT - 1) * E:NT * E], ALU.add))
            v.tensor_reduce(weight, view(ps_m[:], TE, [[1, E], [E, NT]]), AX_X, ALU.add)
            do(v.tensor_scalar(inv, count, 1.0, None, ALU.max))
            do(v.reciprocal(inv, inv))
            do(v.tensor_tensor(weight, weight, inv, ALU.mult))
            full = view(work[:], 0, [[NT, E], [1, NT]])
            do(v.tensor_scalar(inv, count, 1.0 / P, None, ALU.mult))
            do(v.tensor_tensor(full, bc(inv, NT), view(cst[:], C_IOTA, [[0, E], [1, NT]]), ALU.is_gt))
            do(v.tensor_reduce(ntile, full, AX_X, ALU.add))
            pair = view(work[:], 0, [[E, E], [1, E]])
            do(v.tensor_tensor(pair, view(cst[:], C_LOW, [[E, E], [1, E]]), view(ntile, 0, [[0, E], [1, E]]), ALU.mult))
            do(v.tensor_reduce(tstart, pair, AX_X, ALU.add))
            v.tensor_copy(tstart_i[:], tstart[0:1])
            do(v.tensor_tensor(tend, tstart, ntile, ALU.add))
            tile_e = view(work[:], 0, [[E, NTILE], [1, E]])
            expert, is_e, first = tile_f[:, 0], tile_f[:, 1], tile_f[:, 2]
            do(v.tensor_tensor(tile_e, view(cst[:], C_IOTA, [[1, NTILE], [0, E]]), view(tend, 0, [[0, NTILE], [1, E]]),
                               ALU.is_ge))
            do(v.tensor_reduce(expert, tile_e, AX_X, ALU.add))
            do(v.tensor_scalar(expert, expert, float(E - 1), None, ALU.min))
            v.tensor_copy(eid[:], expert[0:1])
            do(v.tensor_tensor(tile_e, view(cst[:], C_IOTA, [[0, NTILE], [1, E]]), bc(expert, E), ALU.is_equal))
            do(v.tensor_tensor(tile_e, tile_e, view(weight, 0, [[0, NTILE], [1, E]]), ALU.mult))
            do(v.tensor_reduce(wt[:], tile_e, AX_X, ALU.add))
            do(v.tensor_tensor(slot[:], before[:], ps_c[:, 0:TE].rearrange("p (t e) -> p t e", e=E), ALU.add))
            do(v.tensor_scalar(inv, tstart, float(P), None, ALU.mult))
            do(v.tensor_tensor(slot[:], slot[:], view(inv, 0, [[0, NT], [1, E]]), ALU.add))
            for k in range(TOPK):
                do(v.scalar_tensor_tensor(ex[:], rank[:], float(k), slot[:], ALU.is_equal, ALU.mult))
                do(v.tensor_reduce(slot3[:, k], ex[:], AX_X, ALU.add))
            s_all, s_tile, s_place = (slot3_i[:, i] for i in range(3))
            f_tile, f_place = slot3_f[:, 0], slot3_f[:, 1]
            do(v.tensor_copy(s_all, slot3[:].rearrange("p k t -> p (k t)")))
            v.tensor_single_scalar(s_tile, s_all, 7, ALU.arith_shift_right)
            do(v.tensor_single_scalar(s_place, s_all, P - 1, ALU.bitwise_and))
            v.tensor_copy(f_tile, s_tile)
            do(v.tensor_copy(f_place, s_place))
            for k in range(TOPK):
                if k > 1:
                    dve.wait_ge(hot_used, k - 1)
                oc, oa = one_hots(work, k, ONE_HOT)
                oc = oc.rearrange("p (t c) -> p t c", t=NT)
                oa = oa.rearrange("p (t c) -> p t c", t=NT)
                v.tensor_tensor(oc, view(cst[:], C_IOTA, [[0, NT], [1, P]]),
                                bc(f_place[:, k * NT:(k + 1) * NT], P), ALU.is_equal)
                do(v.tensor_tensor(oa, view(cst[:], C_IOTA, [[0, NT], [1, NTILE]]),
                                   bc(f_tile[:, k * NT:(k + 1) * NT], NTILE), ALU.is_equal))
                v.tensor_tensor(oa, oa, bc(cst[:, C_TOK:C_TOK + NT], NTILE), ALU.mult).then_inc(hot_ready, 1)
            dve.wait_ge(hot_used, TOPK)
            m = ps_r[:, 0, 0:NTILE]
            used, tok = is_e, first
            trash = cst[:, C_TRASH:C_TRASH + 1]
            v.tensor_scalar(used, m, 0.5, None, ALU.is_gt)
            do(v.tensor_scalar(tok, m, -1.0, 0.0, ALU.add, ALU.max))
            v.tensor_copy(gidx[:], tok)
            do(v.tensor_scalar(expert, tok, trash, None, ALU.subtract))
            do(v.tensor_tensor(expert, expert, used, ALU.mult))
            do(v.tensor_scalar(expert, expert, trash, None, ALU.add))
            v.tensor_copy(sidx[:], expert)


def one_hots(work, k, size):
    at = (k % 2) * size
    return work[:, at:at + NT * P], work[:, at + NT * P:at + size]


def experts(nc, cst, w_hi, w_lo, stage, stage_in, split_done, wcat, b2, b2_sb, b2_in, b1_sb, xnd, acc, tabs):
    gidx, sidx, wt, eid, tstart_i = tabs
    with ExitStack() as ctx:
        def sb(name, shape, dt=F32):
            return ctx.enter_context(nc.sbuf_tensor(name, shape, dt))

        def psum(name, shape):
            return ctx.enter_context(nc.psum_tensor(name, shape, F32))

        def sem(name):
            return ctx.enter_context(nc.semaphore(name))

        gi = sb("gi", [P, 2], U32)
        si = sb("si", [P, 2], U32)
        tick = sb("tick", [P, 5])
        turn = sb("turn", [P, 1])
        b1_now = sb("b1_now", [P, KF])
        xg = sb("xg", [P, 2, D])
        xf = sb("xf", [P, KD * P])
        xh = sb("xh", [P, KD * P], F32R)
        xl = sb("xl", [P, KD * P], F32R)
        h = sb("h", [P, FF])
        hf = sb("hf", [P, FF])
        hh = sb("hh", [P, FF], F32R)
        hl = sb("hl", [P, FF], F32R)
        y = sb("y", [P, 2, D])
        ps_x = psum("ps_xd", [P, 512])
        ps_h = psum("ps_h", [P, 3, 512])
        ps_t = psum("ps_td", [P, 3, 512])
        ps_y = psum("ps_y", [P, 512])
        CHUNKS = [(0, 512), (512, 1024), (1024, FF)]

        gi_ready, si_ready = sem("gi_ready"), sem("si_ready")
        g_in = [sem("g_in0"), sem("g_in1")]
        x_done = sem("x_done")
        xh_ready = sem("xh_ready")
        xl_ready = sem("xl_ready")
        h_done = sem("h_done")
        h_evac = sem("h_evac")
        t_done = sem("t_done")
        b1_ready = sem("b1_ready")
        relu_done = sem("relu_done")
        hh_ready = sem("hh_ready")
        hl_ready = sem("hl_ready")
        y_done = sem("y_done")
        y_evac = sem("y_evac")
        y_biased = sem("y_biased")
        y_ready = sem("y_ready")
        added = sem("added")
        w_rounded = sem("w_rounded")

        block = ctx.enter_context(nc.Block())

        def slot_is_free(eng, e):
            return eng.snap(eng.value_load(tstart_i[0:1, bass.ds(e - 1, 1)], min_val=0, max_val=NTILE) + 1)

        @block.sync
        def _(sp):
            def load(e, slot):
                n = slot_is_free(sp, e)
                row = sp.snap(e * D) if not isinstance(e, int) else e * D
                before = sp.snap(e * 16) if not isinstance(e, int) else e * 16
                with sp.Fori(0, NCHUNK // 2) as c:
                    for par in range(2):
                        at = sp.snap(e * (P * WS) + (2 * c + par) * WC)
                        split = sp.snap(e * NCHUNK + 2 * c + par - 1)
                        sp.wait_ge(split_done, split)
                        sp.dma_start(stage[:, par], bass.AP(tensor=wcat.tensor, offset=at, ap=[[WS, P], [1, WC]]))\
                            .then_inc(stage_in[par], 16)
                sp.wait_ge(y_ready, n)
                sp.wait_ge(b2_in, before)
                sp.dma_start(b2_sb[:, slot], bass.AP(tensor=b2.tensor, offset=row, ap=[[0, P], [1, D]]))\
                    .then_inc(b2_in, 16)

            with sp.Fori(0, E // 2 - 1) as i:
                load(2 * i + 1, 1)
                load(2 * i + 2, 0)
            load(E - 1, 1)
            sp.wait_ge(b2_in, 16 * E)

        @block.vector
        def _(dve):
            with dve.Fori(1, E) as e:
                dve.wait_ge(y_ready, slot_is_free(dve, e))
                nc.vector.tensor_tensor(turn[:], wt[:, 0:1], wt[:, 0:1], ALU.add)
                with dve.Fori(0, NCHUNK // 2) as c:
                    for par in range(2):
                        n = e * NCHUNK + 2 * c + par
                        at = (e % 2) * WS + (2 * c + par) * WC
                        hi, lo = (view(w[:], at, [[1, WC]]) for w in (w_hi, w_lo))
                        dve.wait_ge(stage_in[par], e * (8 * NCHUNK) + 16 * c + 16)
                        nc.vector.tensor_copy(hi, stage[:, par]).then_inc(w_rounded, 1)
                        dve.wait_ge(w_rounded, n - NCHUNK + 1)
                        nc.vector.tensor_tensor(lo, stage[:, par], hi.bitcast(F32), ALU.subtract)\
                            .then_inc(split_done, 1)

        @block.gpsimd
        def _(pool):
            pool.sem_inc(xl_ready, 1)
            pool.sem_inc(hl_ready, 1)
            pool.sem_inc(y_ready, 1)

            def settle(k):
                nc.gpsimd.tensor_tensor(tick[:, k:k + 1], wt[:, 0:1], wt[:, 0:1], ALU.add)

            def gather(i, par):
                nc.gpsimd.tensor_copy(gi[:, par:par + 1], gidx[:, bass.ds(i, 1)]).then_inc(gi_ready, 1)
                pool.wait_ge(gi_ready, i + 1)
                settle(0)
                pool.indirect_dma_start(xg[:, par], None, xnd,
                                        bass.IndirectOffsetOnAxis(ap=gi[:, par:par + 1], axis=0))\
                    .then_inc(g_in[par], 16)

            def x_lo(i):
                pool.wait_ge(xh_ready, i + 2)
                nc.gpsimd.tensor_tensor(xl[:], xf[:], xh[:].bitcast(F32), ALU.subtract).then_inc(xl_ready, 1)

            def h_lo(i):
                pool.wait_ge(hh_ready, i + 1)
                nc.gpsimd.tensor_tensor(hl[:], hf[:], hh[:].bitcast(F32), ALU.subtract).then_inc(hl_ready, 1)

            def result(i, par, later):
                e = pool.value_load(eid[0:1, bass.ds(i, 1)], min_val=0, max_val=E - 1)
                pool.wait_ge(b2_in, e * 16 + 16)
                settle(1)
                pool.wait_ge(y_evac, i + 2)
                nc.gpsimd.tensor_tensor(y[:, par], y[:, par], view(b2_sb[:], (e % 2) * D, [[1, D]]), ALU.add)\
                    .then_inc(y_biased, 1)
                pool.wait_ge(y_biased, i + 1)
                nc.gpsimd.tensor_tensor(y[:, par], y[:, par], view(wt[:], i, [[0, D]]), ALU.mult)\
                    .then_inc(y_ready, 1)
                nc.gpsimd.tensor_copy(si[:, par:par + 1], sidx[:, bass.ds(i, 1)]).then_inc(si_ready, 1)
                pool.wait_ge(si_ready, i + 1)
                settle(2)
                pool.wait_ge(y_ready, i + 2)
                settle(3)
                if later:
                    pool.wait_ge(added, 16 * i)
                    settle(4)
                pool.indirect_dma_start(acc, bass.IndirectOffsetOnAxis(ap=si[:, par:par + 1], axis=0),
                                        y[:, par], None, compute_op=ALU.add).then_inc(added, 16)

            def tile(i, par, gather_next=True, x_next=True, later=True):
                h_lo(i)
                if gather_next:
                    pool.wait_ge(x_done, i + 2)
                    gather(i + 3, 1 - par)
                if x_next:
                    x_lo(i + 2)
                result(i, par, later)

            gather(0, 0)
            gather(1, 1)
            x_lo(0)
            pool.wait_ge(x_done, 1)
            gather(2, 0)
            x_lo(1)
            tile(0, 0, later=False)
            tile(1, 1)
            with pool.Fori(1, NTILE // 2 - 2) as j:
                tile(2 * j, 0)
                tile(2 * j + 1, 1)
            for i in range(NTILE - 4, NTILE):
                tile(i, i % 2, i + 3 < NTILE, i + 2 < NTILE)
            pool.wait_ge(added, 16 * NTILE)

        @block.scalar
        def _(act):
            act.sem_inc(xh_ready, 1)
            act.sem_inc(relu_done, 1)
            act.sem_inc(y_evac, 1)

            def evac_x(i):
                act.wait_ge(x_done, i + 1)
                act.wait_ge(xl_ready, i + 1)
                nc.scalar.activation(xf[:], ps_x[:], ACT.Copy)
                nc.scalar.activation(xh[:], ps_x[:], ACT.Copy).then_inc(xh_ready, 1)

            def evac_h(i):
                for c, (lo, hi) in enumerate(CHUNKS):
                    act.wait_ge(h_done, 3 * i + c + 1)
                    nc.scalar.activation(h[:, lo:hi], ps_h[:, c, 0:hi - lo], ACT.Copy).then_inc(h_evac, 1)

            def hidden(i):
                e = act.value_load(eid[0:1, bass.ds(i, 1)], min_val=0, max_val=E - 1)
                nc.scalar.activation(b1_now[:], b1_sb[:, bass.ds(e * KF, KF)], ACT.Copy).then_inc(b1_ready, 1)
                act.wait_ge(b1_ready, i + 1)
                act.wait_ge(t_done, i + 1)
                act.wait_ge(hl_ready, i + 1)
                for k in range(KF):
                    last = nc.scalar.activation(hf[:, k * P:(k + 1) * P], ps_t[:, k // 4, (k % 4) * P:(k % 4 + 1) * P],
                                                ACT.Relu, bias=b1_now[:, k:k + 1])
                last.then_inc(relu_done, 1)
                act.wait_ge(relu_done, i + 2)
                nc.scalar.activation(hh[:], hf[:], ACT.Copy).then_inc(hh_ready, 1)

            def evac_y(i, par, later):
                act.wait_ge(y_done, i + 1)
                if later:
                    act.wait_ge(added, 16 * i - 16)
                nc.scalar.activation(y[:, par], ps_y[:], ACT.Copy).then_inc(y_evac, 1)

            def tile(i, par, w1_next=True, x_next=True, later=True):
                hidden(i)
                if w1_next:
                    evac_h(i + 1)
                if x_next:
                    evac_x(i + 2)
                evac_y(i, par, later)

            evac_x(0)
            evac_h(0)
            evac_x(1)
            tile(0, 0, later=False)
            tile(1, 1, later=False)
            with act.Fori(1, NTILE // 2 - 1) as j:
                tile(2 * j, 0)
                tile(2 * j + 1, 1)
            tile(NTILE - 2, 0, True, False)
            tile(NTILE - 1, 1, False, False)

        @block.tensor
        def _(pe):
            ident = cst[:, C_ID:C_ID + P]

            def expert_of(i):
                return pe.value_load(eid[0:1, bass.ds(i, 1)], min_val=0, max_val=E - 1)

            def x_t(i, j, par):
                pe.wait_ge(g_in[par], 16 * j + 16)
                pe.wait_ge(xh_ready, i + 1)
                for k in range(KD):
                    last = nc.tensor.transpose(ps_x[:, k * P:(k + 1) * P], xg[:, par, k * P:(k + 1) * P], ident)
                last.then_inc(x_done, 1)

            def part(w, e, at, n):
                return view(w[:], (e % 2) * WS + at, [[1, n]])

            def first_product(i, e, first):
                pe.wait_ge(split_done, e * NCHUNK + NCHUNK)
                pe.wait_ge(xh_ready, i + 2)
                for c, (lo, hi) in enumerate(CHUNKS):
                    out = ps_h[:, c, 0:hi - lo]
                    if not first:
                        pe.wait_ge(h_evac, 3 * i + c - 2)
                    for k in range(KD):
                        x_hi = xh[:, k * P:(k + 1) * P]
                        nc.tensor.matmul(out, x_hi, part(w_hi, e, k * FF + lo, hi - lo), start=(k == 0), stop=False)
                        nc.tensor.matmul(out, x_hi, part(w_lo, e, k * FF + lo, hi - lo), start=False, stop=False)
                    if c == 0:
                        pe.wait_ge(xl_ready, i + 2)
                    for k in range(KD):
                        last = nc.tensor.matmul(out, xl[:, k * P:(k + 1) * P], part(w_hi, e, k * FF + lo, hi - lo),
                                                start=False, stop=(k == KD - 1))
                    last.then_inc(h_done, 1)

            def h_t(i):
                pe.wait_ge(h_evac, 3 * i + 3)
                pe.wait_ge(relu_done, i + 1)
                for k in range(KF):
                    last = nc.tensor.transpose(ps_t[:, k // 4, (k % 4) * P:(k % 4 + 1) * P],
                                               h[:, k * P:(k + 1) * P], ident)
                last.then_inc(t_done, 1)

            def second_product(i, e):
                pe.wait_ge(hh_ready, i + 1)
                pe.wait_ge(y_evac, i + 1)
                for k in range(KF):
                    h_hi = hh[:, k * P:(k + 1) * P]
                    nc.tensor.matmul(ps_y[:], h_hi, part(w_hi, e, KD * FF + k * D, D), start=(k == 0), stop=False)
                    nc.tensor.matmul(ps_y[:], h_hi, part(w_lo, e, KD * FF + k * D, D), start=False, stop=False)
                pe.wait_ge(hl_ready, i + 2)
                for k in range(KF):
                    last = nc.tensor.matmul(ps_y[:], hl[:, k * P:(k + 1) * P], part(w_hi, e, KD * FF + k * D, D),
                                            start=False, stop=(k == KF - 1))
                last.then_inc(y_done, 1)

            def tile(i, j, par, w1_next, x_next):
                h_t(i)
                if w1_next:
                    first_product(i + 1, expert_of(i + 1), False)
                if x_next:
                    x_t(i + 2, j + 1, par)
                second_product(i, expert_of(i))

            x_t(0, 0, 0)
            first_product(0, expert_of(0), True)
            x_t(1, 0, 1)
            with pe.Fori(0, NTILE // 2 - 1) as j:
                tile(2 * j, j, 0, True, True)
                tile(2 * j + 1, j, 1, True, True)
            tile(NTILE - 2, None, 0, True, False)
            tile(NTILE - 1, None, 1, False, False)


def finish(nc, cst, x2d, acc, wp1, bp1, wp2, bp2, out):
    PH = wp1.shape[1]
    KP = PH // P
    with ExitStack() as ctx:
        def sb(name, shape, dt=F32):
            return ctx.enter_context(nc.sbuf_tensor(name, shape, dt))

        def sem(name):
            return ctx.enter_context(nc.semaphore(name))

        xs = sb("x2_sb", [P, NT, D])
        o = sb("o_sb", [P, NT, D])
        wp1_sb = sb("wp1_sb", [P, KD, PH])
        bp1_sb = sb("bp1_sb", [P, KP])
        wp2_sb = sb("wp2_sb", [P, KP])
        wp2_b = sb("wp2_b", [P, KP, P])
        bp2_sb = sb("bp2_sb", [P, 1])
        pooled = sb("pooled", [P, KD * B])
        hid = sb("hid", [P, KP, B])
        z = sb("z", [P, B])
        ps_pool = ctx.enter_context(nc.psum_tensor("ps_pool", [P, 512], F32))
        ps_hid = ctx.enter_context(nc.psum_tensor("ps_hid", [P, 512], F32))
        ps_z = ctx.enter_context(nc.psum_tensor("ps_z", [P, 512], F32))
        small_in = sem("small_in_e")
        x_in = [sem(f"x2_in{i}") for i in range(4)]
        o_in = [sem(f"o_in{i}") for i in range(4)]
        pooled_done, pooled_ready, wide, hid_done, hid_ready, z_done, z_ready, e_ready, step, gated, stored = (
            sem(n) for n in ("pooled_done", "pooled_ready", "wide", "hid_done", "hid_ready", "z_done", "z_ready",
                             "e_ready", "step_e", "gated", "stored"))
        block = ctx.enter_context(nc.Block())

        @block.sync
        def _(sp):
            src = acc.rearrange("(t p) d -> p t d", p=P)
            for i in range(4):
                sp.dma_start(o[:, 4 * i:4 * i + 4], src[:, 4 * i:4 * i + 4]).then_inc(o_in[i], 16)
            src = x2d.rearrange("(t p) d -> p t d", p=P)
            for i in range(4):
                sp.dma_start(xs[:, 4 * i:4 * i + 4], src[:, 4 * i:4 * i + 4]).then_inc(x_in[i], 16)
            dst = out.rearrange("b (t p) d -> p (b t) d", p=P)
            for i in range(B):
                sp.wait_ge(gated, 2 * i + 2)
                sp.dma_start(dst[:, 2 * i:2 * i + 2], o[:, 2 * i:2 * i + 2]).then_inc(stored, 16)
            sp.wait_ge(stored, 16 * B)

        @block.scalar
        def _(act):
            act.dma_start(wp1_sb[:], wp1.rearrange("(k p) n -> p k n", p=P)).then_inc(small_in, 16)
            act.dma_start(bp1_sb[:], bp1).then_inc(small_in, 16)
            act.dma_start(wp2_sb[:], wp2).then_inc(small_in, 16)
            act.dma_start(bp2_sb[:], bp2.partition_broadcast(P)).then_inc(small_in, 16)
            act.wait_ge(small_in, 64)
            act.wait_ge(pooled_done, 1)
            nc.scalar.activation(pooled[:], ps_pool[:, 0:KD * B], ACT.Copy, scale=1.0 / S).then_inc(pooled_ready, 1)
            act.wait_ge(hid_done, 1)
            for c in range(KP):
                last = nc.scalar.activation(hid[:, c], ps_hid[:, c * B:(c + 1) * B], ACT.Relu, bias=bp1_sb[:, c:c + 1])
            last.then_inc(hid_ready, 1)
            act.wait_ge(z_ready, 1)
            nc.scalar.activation(z[:], z[:], ACT.Exp, scale=-1.0).then_inc(e_ready, 1)

        @block.tensor
        def _(pe):
            for b in range(B):
                if b % 2 == 0:
                    pe.wait_ge(o_in[b // 2], 16)
                for k in range(KD):
                    for t in range(TPB):
                        last = nc.tensor.matmul(ps_pool[:, k * B + b:k * B + b + 1],
                                                o[:, 2 * b + t, k * P:(k + 1) * P], cst[:, C_ONE:C_ONE + 1],
                                                start=(t == 0), stop=(t == TPB - 1))
            last.then_inc(pooled_done, 1)
            pe.wait_ge(small_in, 64)
            pe.wait_ge(pooled_ready, 1)
            for c in range(KP):
                for k in range(KD):
                    last = nc.tensor.matmul(ps_hid[:, c * B:(c + 1) * B], wp1_sb[:, k, c * P:(c + 1) * P],
                                            pooled[:, k * B:(k + 1) * B], start=(k == 0), stop=(k == KD - 1))
            last.then_inc(hid_done, 1)
            pe.wait_ge(wide, 1)
            pe.wait_ge(hid_ready, 1)
            for c in range(KP):
                last = nc.tensor.matmul(ps_z[:, 0:B], wp2_b[:, c], hid[:, c], start=(c == 0), stop=(c == KP - 1))
            last.then_inc(z_done, 1)

        @block.vector
        def _(dve):
            do = Steps(dve, step).do
            dve.wait_ge(small_in, 64)
            nc.vector.tensor_copy(wp2_b[:], bc(wp2_sb[:], P)).then_inc(wide, 1)
            dve.wait_ge(z_done, 1)
            nc.vector.tensor_scalar(z[:], ps_z[:, 0:B], bp2_sb[:], None, ALU.add).then_inc(z_ready, 1)
            dve.wait_ge(e_ready, 1)
            do(nc.vector.tensor_scalar(z[:], z[:], 1.0, None, ALU.add))
            do(nc.vector.reciprocal(z[:], z[:]))
            do(nc.vector.tensor_scalar(z[:], z[:], 0.7, -0.8, ALU.is_gt, ALU.mult))
            do(nc.vector.tensor_scalar(z[:], z[:], 1.0, None, ALU.add))
            for i in range(4):
                dve.wait_ge(o_in[i], 16)
                dve.wait_ge(x_in[i], 16)
                with dve.Fori(2 * i, 2 * i + 2) as b:
                    for t in range(TPB):
                        nc.vector.scalar_tensor_tensor(o[:, 2 * b + t], o[:, 2 * b + t], z[:, bass.ds(b, 1)],
                                                       xs[:, 2 * b + t], ALU.mult, ALU.add).then_inc(gated, 1)


def decoder_layer(nc, out, **a):
    with ExitStack() as ctx:
        def sb(stack, name, shape, dt=F32):
            return stack.enter_context(nc.sbuf_tensor(name, shape, dt))

        cst = sb(ctx, "cst", [P, NCONST])
        tabs = (sb(ctx, "gidx", [P, NTILE], U32), sb(ctx, "sidx", [P, NTILE], U32), sb(ctx, "wt", [P, NTILE]),
                sb(ctx, "eid", [1, NTILE], I32), sb(ctx, "tstart_i", [1, E], I32))
        b1_sb = sb(ctx, "b1_sb", [P, E * KF])
        kpad = nc.dram_tensor("kpad", (SH, KPAD), F32, kind="Internal").ap()
        x2d = nc.dram_tensor("x2d", (NT * P, D), F32, kind="Internal").ap()
        xnd = nc.dram_tensor("xnd", (NT * P, D), F32, kind="Internal").ap()
        acc = nc.dram_tensor("acc", (NT * P + P, D), F32, kind="Internal").ap()
        with ExitStack() as mid:
            prob = sb(mid, "prob", [P, NT, E])
            with ExitStack() as early:
                xs = sb(early, "xs", [P, NT, D])
                stats1 = sb(early, "stats1", [P, NT, 6])
                attention(nc, xs, cst, a["x"], a["L0_attn_Wq"], a["L0_attn_Wk"], a["L0_attn_Wv"], a["L0_attn_Wo"],
                          a["L0_attn_bq"], a["L0_attn_bk"], a["L0_attn_bv"], a["L0_attn_bo"], a["consts"], stats1)
                res = sb(early, "res", [P, LB * B * S])
                convolution(nc, xs, cst, stats1, res, a["ctx_rev"], a["L0_xattn_ssm_kernel"], a["L0_xattn_D"], kpad)
                logits_phase(nc, xs, cst, res, prob, a["L0_ffn_Wr"], a["L0_ffn_br"], a["L0_ffn_b1"], b1_sb,
                             x2d, xnd, acc)
            with ExitStack() as late:
                def right(name, shape, dt=F32):
                    return late.enter_context(nc.sbuf_tensor(name, shape, dt, side="right"))

                w_hi = right("w_hi", [P, 2, WS], F32R)
                w_lo = right("w_lo", [P, 2, WS], F32R)
                stage = right("stage", [P, 2, WC])
                b2_sb = right("b2_sb", [P, 2, D])
                stage_in = [late.enter_context(nc.semaphore(f"stage_in{i}")) for i in range(2)]
                split_done = late.enter_context(nc.semaphore("split_done"))
                b2_in = late.enter_context(nc.semaphore("b2_in"))
                route(nc, cst, prob, w_hi, w_lo, stage, stage_in, split_done, a["wcat"], a["L0_ffn_b2"], b2_sb,
                      b2_in, tabs)
                experts(nc, cst, w_hi, w_lo, stage, stage_in, split_done, a["wcat"], a["L0_ffn_b2"], b2_sb, b2_in,
                        b1_sb, xnd, acc, tabs)
        finish(nc, cst, x2d, acc, a["L0_ffn_Wp1"], a["L0_ffn_bp1"], a["L0_ffn_Wp2"], a["L0_ffn_bp2"], out)


def const_table():
    import numpy as np
    c = np.zeros((P, NCONST), np.float32)
    p = np.arange(P)
    c[:, C_ID:C_ID + P] = p[:, None] == p[None]
    c[:, C_UP:C_UP + P] = p[:, None] < p[None]
    c[:, C_ONE:C_ONE + P] = 1
    c[:, C_IOTA:C_IOTA + P] = p[None]
    theta = (np.float32(1.0) / np.float32(10000.0) ** (np.arange(0, HD, 2, dtype=np.float32) / np.float32(HD)))
    key_pos = np.where(p < START, p, S - NK + p)
    for j, pos in enumerate((p, P + p, key_pos)):
        angle = (pos.astype(np.float32)[:, None] * theta[None]).astype(np.float32)
        c[:, C_ROPE + j * HD:C_ROPE + j * HD + HD // 2] = np.cos(angle)
        c[:, C_ROPE + j * HD + HD // 2:C_ROPE + (j + 1) * HD] = np.sin(angle)
    e = np.arange(E)
    c[:, C_LOW:C_LOW + E * E] = (e[None, :] < e[:, None]).reshape(1, E * E)
    c[:, C_TOK:C_TOK + NT] = 1 + p[:, None] + P * np.arange(NT)[None]
    c[:, C_TRASH] = TRASH + p
    return c


def kernel(**inputs):
    import numpy as _np
    import concourse.bacc as _bacc
    from concourse import mybir as _mybir
    from concourse.bass_utils import run_bass_kernel_spmd as _run

    arrays = {n: _np.ascontiguousarray(a) for n, a in inputs.items()}
    for n in ("Wq", "Wk", "Wv", "Wo"):
        arrays[f"L0_attn_{n}"] = _np.ascontiguousarray(arrays[f"L0_attn_{n}"].T)
    c = arrays.pop("ctx_2048").reshape(B, SH, CH, LB, P)[..., ::-1].transpose(1, 4, 3, 0, 2)
    arrays["ctx_rev"] = _np.ascontiguousarray(_np.concatenate([c, c[..., :CE - CH]], axis=-1)).reshape(SH, P, -1)
    arrays["L0_ffn_b1"] = _np.ascontiguousarray(arrays["L0_ffn_b1"].reshape(E, KF, P).transpose(2, 0, 1)).reshape(P, -1)
    for n in ("bp1", "Wp2"):
        arrays[f"L0_ffn_{n}"] = _np.ascontiguousarray(arrays[f"L0_ffn_{n}"].reshape(-1, P).T)
    w1 = arrays.pop("L0_ffn_w1").reshape(E, KD, P, FF).transpose(0, 2, 1, 3).reshape(E, P, KD * FF)
    w2 = arrays.pop("L0_ffn_w2").reshape(E, KF, P, D).transpose(0, 2, 1, 3).reshape(E, P, KF * D)
    arrays["wcat"] = _np.concatenate([w1, w2], axis=-1)
    arrays["consts"] = const_table()

    nc = _bacc.Bacc("TRN2", target_bir_lowering=False, num_devices=1)
    feeds, args = {}, {}
    for n, a in arrays.items():
        feeds[f"in_{n}"] = a
        args[n] = nc.dram_tensor(f"in_{n}", a.shape, _mybir.dt.from_np(a.dtype), kind="ExternalInput").ap()
    out = nc.dram_tensor("out_0", (B, S, D), F32, kind="ExternalOutput").ap()
    decoder_layer(nc, out, **args)
    r = _run(nc, [feeds], core_ids=[0])
    return r.results[0]["out_0"]
```
